# Optimizing a Trainium2 kernel written in Bass

```python
import numpy as np
import jax
import jax.numpy as jnp

def _softmax(x, axis=-1):
    return jax.nn.softmax(x, axis=axis)

def _gelu(x):
    return jax.nn.gelu(x, approximate=True)

def _silu(x):
    return jax.nn.silu(x)

def _sigmoid(x):
    return jax.nn.sigmoid(x)

def _layernorm(x, axis=-1, eps=1e-05):
    m = jnp.mean(x, axis=axis, keepdims=True)
    v = jnp.var(x, axis=axis, keepdims=True)
    return (x - m) / jnp.sqrt(v + eps)

def _scatter_add(tgt, idx, src, axis=0):
    return tgt.at[idx].add(src)

def _segment_sum(src, seg, n):
    return jax.ops.segment_sum(src, seg, n)
kernel_name = 'mk_xattn_ffn_d1_seqx_r4_4ace4d'

def setup_inputs(seed: int=0):
    np.random.seed(seed)
    _w = jnp.asarray

    def _rec_inputs():
        import jax
        import jax.numpy as jnp
        _rk = jax.random.key(seed)
        x = -0.0003929 + 0.9999 * jax.random.normal(jax.random.fold_in(_rk, 1), (32, 100, 256), jnp.float32)
        _lenS = 100 - jax.random.randint(jax.random.fold_in(_rk, 7), (32,), 0, max(1, 100 // 4) + 1, jnp.int32)
        _lenS2 = 361 - jax.random.randint(jax.random.fold_in(_rk, 8), (32,), 0, max(1, 361 // 4) + 1, jnp.int32)
        _ctx_768P = jax.random.normal(jax.random.fold_in(_rk, 11), (32, 16, 192), jnp.float32)
        _ctx_768c = jax.random.dirichlet(jax.random.fold_in(_rk, 511), 0.3 * jnp.ones((16,), jnp.float32), (32, 361))
        _ctx_768t = jnp.einsum('bsk,bkd->bsd', _ctx_768c, _ctx_768P)
        _ctx_768t = _ctx_768t * jax.lax.rsqrt(jnp.mean(jnp.square(_ctx_768t)) + 1e-12) * 0.953939
        ctx_768 = -7.36909e-05 + 0.999899 * (_ctx_768t + 0.3 * jax.random.normal(jax.random.fold_in(_rk, 611), (32, 361, 192), jnp.float32))
        return (x, ctx_768)
    x, ctx_768 = _rec_inputs()

    def _L0_xattn_setup():
        import jax, jax.numpy as jnp
        import numpy as np
        EPS = 1e-05

        def layernorm(x, g, b):
            mu = jnp.mean(x, axis=-1, keepdims=True)
            var = jnp.mean(jnp.square(x - mu), axis=-1, keepdims=True)
            return (x - mu) * jax.lax.rsqrt(var + EPS) * g + b
        key = jax.random.key(seed)
        ks = jax.random.split(key, 12)
        B, L1, L2 = (8, 512, 512)
        D1, D2, E = (256, 192, 256)
        s1, s2, se = (D1 ** (-0.5), D2 ** (-0.5), E ** (-0.5))
        return {'modality1': jax.random.normal(ks[0], (B, L1, D1), jnp.float32), 'modality2': jax.random.normal(ks[1], (B, L2, D2), jnp.float32), 'ln1_g': jnp.ones((D1,), jnp.float32), 'ln1_b': jnp.zeros((D1,), jnp.float32), 'ln2_g': jnp.ones((D2,), jnp.float32), 'ln2_b': jnp.zeros((D2,), jnp.float32), 'Wq': jax.random.normal(ks[2], (D1, E), jnp.float32) * s1, 'bq': jax.random.normal(ks[3], (E,), jnp.float32) * 0.01, 'Wk': jax.random.normal(ks[4], (D2, E), jnp.float32) * s2, 'bk': jax.random.normal(ks[5], (E,), jnp.float32) * 0.01, 'Wv': jax.random.normal(ks[6], (D2, E), jnp.float32) * s2, 'bv': jax.random.normal(ks[7], (E,), jnp.float32) * 0.01, 'Wo': jax.random.normal(ks[8], (E, D1), jnp.float32) * se, 'bo': jax.random.normal(ks[9], (D1,), jnp.float32) * 0.01}
    _L0_xattn_all = _L0_xattn_setup()
    _L0_xattn_in = {k: v for k, v in _L0_xattn_all.items() if k in ('ln1_g', 'ln1_b', 'ln2_g', 'ln2_b', 'Wq', 'bq', 'Wk', 'bk', 'Wv', 'bv', 'Wo', 'bo')}
    del _L0_xattn_all

    def _L0_ffn_setup():
        import jax, jax.numpy as jnp
        import numpy as np
        B, S, DIM = (4, 512, 256)
        INTER = int(int(DIM * 4) * 0.25)
        E = 32 - 1
        K = 4 - 1

        def _gelu(t):
            return jax.nn.gelu(t, approximate=False)
        key = jax.random.key(seed)
        ks = jax.random.split(key, 12)
        s = 0.02
        return {'x': jax.random.normal(ks[0], (B, S, DIM), jnp.float32), 'ws1': jax.random.normal(ks[1], (DIM, INTER), jnp.float32) * s, 'bs1': jnp.zeros((INTER,), jnp.float32), 'ws2': jax.random.normal(ks[2], (INTER, DIM), jnp.float32) * s, 'bs2': jnp.zeros((DIM,), jnp.float32), 'We1': jax.random.normal(ks[3], (E, DIM, INTER), jnp.float32) * s, 'Be1': jnp.zeros((E, INTER), jnp.float32), 'We2': jax.random.normal(ks[4], (E, INTER, DIM), jnp.float32) * s, 'Be2': jnp.zeros((E, DIM), jnp.float32), 'Wr': jax.random.normal(ks[5], (DIM, E), jnp.float32) * s, 'br': jnp.zeros((E,), jnp.float32)}
    _L0_ffn_all = _L0_ffn_setup()
    _L0_ffn_in = {k: v for k, v in _L0_ffn_all.items() if k in ('ws1', 'bs1', 'ws2', 'bs2', 'We1', 'Be1', 'We2', 'Be2', 'Wr', 'br')}
    del _L0_ffn_all
    return {'x': x, 'ctx_768': ctx_768, 'L0_xattn_ln1_g': _L0_xattn_in['ln1_g'], 'L0_xattn_ln1_b': _L0_xattn_in['ln1_b'], 'L0_xattn_ln2_g': _L0_xattn_in['ln2_g'], 'L0_xattn_ln2_b': _L0_xattn_in['ln2_b'], 'L0_xattn_Wq': _L0_xattn_in['Wq'], 'L0_xattn_bq': _L0_xattn_in['bq'], 'L0_xattn_Wk': _L0_xattn_in['Wk'], 'L0_xattn_bk': _L0_xattn_in['bk'], 'L0_xattn_Wv': _L0_xattn_in['Wv'], 'L0_xattn_bv': _L0_xattn_in['bv'], 'L0_xattn_Wo': _L0_xattn_in['Wo'], 'L0_xattn_bo': _L0_xattn_in['bo'], 'L0_ffn_ws1': _L0_ffn_in['ws1'], 'L0_ffn_bs1': _L0_ffn_in['bs1'], 'L0_ffn_ws2': _L0_ffn_in['ws2'], 'L0_ffn_bs2': _L0_ffn_in['bs2'], 'L0_ffn_We1': _L0_ffn_in['We1'], 'L0_ffn_Be1': _L0_ffn_in['Be1'], 'L0_ffn_We2': _L0_ffn_in['We2'], 'L0_ffn_Be2': _L0_ffn_in['Be2'], 'L0_ffn_Wr': _L0_ffn_in['Wr'], 'L0_ffn_br': _L0_ffn_in['br']}

def reference(x, ctx_768, L0_xattn_ln1_g, L0_xattn_ln1_b, L0_xattn_ln2_g, L0_xattn_ln2_b, L0_xattn_Wq, L0_xattn_bq, L0_xattn_Wk, L0_xattn_bk, L0_xattn_Wv, L0_xattn_bv, L0_xattn_Wo, L0_xattn_bo, L0_ffn_ws1, L0_ffn_bs1, L0_ffn_ws2, L0_ffn_bs2, L0_ffn_We1, L0_ffn_Be1, L0_ffn_We2, L0_ffn_Be2, L0_ffn_Wr, L0_ffn_br):
    import jax
    import jax.numpy as jnp

    def _L0_xattn_ref(modality1, modality2, ln1_g, ln1_b, ln2_g, ln2_b, Wq, bq, Wk, bk, Wv, bv, Wo, bo):
        import jax, jax.numpy as jnp
        import numpy as np
        EPS = 1e-05

        def layernorm(x, g, b):
            mu = jnp.mean(x, axis=-1, keepdims=True)
            var = jnp.mean(jnp.square(x - mu), axis=-1, keepdims=True)
            return (x - mu) * jax.lax.rsqrt(var + EPS) * g + b
        E = Wq.shape[1]
        scaling = E ** (-0.5)
        x1 = layernorm(modality1, ln1_g, ln1_b)
        x2 = layernorm(modality2, ln2_g, ln2_b)
        q = x1 @ Wq + bq
        k = x2 @ Wk + bk
        v = x2 @ Wv + bv
        scores = jnp.einsum('bqe,bke->bqk', q, k) * scaling
        attn = jax.nn.softmax(scores, axis=-1)
        ctx = jnp.einsum('bqk,bke->bqe', attn, v)
        return ctx @ Wo + bo

    def _L0_ffn_ref(x, ws1, bs1, ws2, bs2, We1, Be1, We2, Be2, Wr, br):
        import jax, jax.numpy as jnp
        import numpy as np
        B, S, DIM = (4, 512, 256)
        INTER = int(int(DIM * 4) * 0.25)
        E = 32 - 1
        K = 4 - 1

        def _gelu(t):
            return jax.nn.gelu(t, approximate=False)
        shared = _gelu(x @ ws1 + bs1) @ ws2 + bs2
        aff = jax.nn.softmax(x @ Wr + br, axis=-1)
        vals, idx = jax.lax.top_k(aff, K)
        gates = jnp.sum(jax.nn.one_hot(idx, E, dtype=x.dtype) * vals[..., None], axis=-2)
        gates_e = jnp.moveaxis(gates, -1, 0)

        def step(acc, p):
            W1, B1, W2, B2, g = p
            h = _gelu(x @ W1 + B1)
            return (acc + g[..., None] * (h @ W2 + B2), None)
        routed, _ = jax.lax.scan(step, jnp.zeros_like(x), (We1, Be1, We2, Be2, gates_e))
        return shared + routed + x
    x = x + _L0_xattn_ref(_layernorm(x, axis=-1), ctx_768, L0_xattn_ln1_g, L0_xattn_ln1_b, L0_xattn_ln2_g, L0_xattn_ln2_b, L0_xattn_Wq, L0_xattn_bq, L0_xattn_Wk, L0_xattn_bk, L0_xattn_Wv, L0_xattn_bv, L0_xattn_Wo, L0_xattn_bo)
    x = x + _L0_ffn_ref(_layernorm(x, axis=-1), L0_ffn_ws1, L0_ffn_bs1, L0_ffn_ws2, L0_ffn_bs2, L0_ffn_We1, L0_ffn_Be1, L0_ffn_We2, L0_ffn_Be2, L0_ffn_Wr, L0_ffn_br)
    return x

_drawn_inputs = setup_inputs


def setup_inputs(seed=0):
    import zlib

    import numpy as np

    out = dict(_drawn_inputs(seed))
    spreads = {'L0_xattn_ln1_g': (1.0, 0.2),
     'L0_xattn_ln1_b': (0.0, 0.43),
     'L0_xattn_ln2_g': (1.0, 0.2),
     'L0_xattn_ln2_b': (0.0, 0.1),
     'L0_ffn_bs1': (0.0, 0.8),
     'L0_ffn_bs2': (0.0, 0.281),
     'L0_ffn_Be1': (0.0, 0.8),
     'L0_ffn_Be2': (0.0, 0.8),
     'L0_ffn_br': (0.0, 0.8)}
    factors = {'L0_xattn_bq': 8.0,
     'L0_xattn_bk': 64.0,
     'L0_xattn_bv': 6.722,
     'L0_xattn_bo': 6.322,
     'L0_ffn_We1': 8.0,
     'L0_ffn_We2': 8.0,
     'L0_ffn_Wr': 8.0,
     'L0_ffn_ws1': 3.004}
    for name, (base, spread) in spreads.items():
        noise = np.random.default_rng([zlib.crc32(name.encode()), seed]).standard_normal(out[name].shape)
        drawn = base * np.exp(spread * noise) if base else spread * noise
        out[name] = jnp.asarray(drawn.astype(out[name].dtype))
    for name, factor in factors.items():
        out[name] = (out[name] * factor).astype(out[name].dtype)
    return out
```

```python
import concourse.bass as bass
from concourse import mybir
from contextlib import ExitStack

F32 = mybir.dt.float32
BF16 = mybir.dt.bfloat16
I32 = mybir.dt.int32
U32 = mybir.dt.uint32
ALU = mybir.AluOpType
ACT = mybir.ActivationFunctionType
AX = mybir.AxisListType

P = 128
B, LQ, LK = 32, 100, 361
D1, D2, E = 256, 192, 256
NE, TOP = 31, 3
INTER = 256
EPS = 1e-5
SCALE = float(E) ** -0.5

D2B = D2 - P
D2C = D2B + 1
KT = [P, P, LK - 2 * P]
TOKENS = B * LQ
SHARED_TILES = TOKENS // P
CAP = TOKENS + P
ROUTED_TILES = (TOKENS * TOP - NE) // P + NE
LIST_END = TOKENS + NE * CAP
REC = NE + 8 + TOP

UN = 4
SLOTS = 4


class At:

    def __init__(self, j, r, n):
        self.j, self.r, self.n = j, r, n
        self.fixed = isinstance(j, int)

    def back(self, k):
        return At(self.j, self.r - k, self.n)

    def count(self, k=0):
        assert self.r + k >= 0
        return self.r + k if self.fixed else self.j * self.n + (self.r + k)

    def has(self, k):
        assert self.fixed or self.r >= k
        return self.r >= k

    def slot(self, m):
        return self.r % m

    def turn(self, m, k=0):
        assert self.r // m + k >= 0
        return self.r // m + k if self.fixed else self.j * (self.n // m) + (self.r // m + k)


def alone(eng):
    eng.nop(nofuse=True)


def walk(eng, step, lo, hi, n, head=0, tail=0):
    for i in range(lo, lo + head):
        step(At(0, i, n))
    passes = (hi - lo - head - tail) // n
    with eng.Fori(0, passes) as j:
        for r in range(lo + head, lo + head + n):
            step(At(j, r, n))
    for i in range(lo + head + n * passes, hi):
        step(At(0, i, n))


def program(nc, x, ctx_t, g1c, b1c, g2c, b2c, wq, wqt, bqc, wk, wkt, bkc, wv, wvt, bvc, wo, bo,
            w1, be1, w2, b2, wr, br, out):
    xs = nc.dram_tensor("expert_rows_in", [LIST_END, D1], F32, kind="Internal").ap()
    ys = nc.dram_tensor("expert_rows_out", [(SHARED_TILES + ROUTED_TILES) * P, D1], F32, kind="Internal").ap()
    base_d = nc.dram_tensor("residual_rows", [B, LQ, D1], F32, kind="Internal").ap()
    tab_d = nc.dram_tensor("tile_table", [ROUTED_TILES, 2], I32, kind="Internal").ap()
    x4 = x.rearrange("(q s) t d -> s q t d", s=SLOTS)
    c4 = ctx_t.rearrange("(q s) t d -> s q t d", s=SLOTS)
    h4 = xs[0:TOKENS, :].rearrange("(q s t) d -> s q t d", s=SLOTS, t=LQ)
    base4 = base_d.rearrange("(q s) t d -> s q t d", s=SLOTS)
    w1_4 = w1.rearrange("(q s) p n -> s q p n", s=SLOTS)
    w2_4 = w2.rearrange("(q s) p n -> s q p n", s=SLOTS)

    stack = ExitStack()
    with stack:
        def sb(name, shape, dt=F32, st=stack):
            return st.enter_context(nc.sbuf_tensor(name, shape, dt))

        def sems(*names):
            return [stack.enter_context(nc.semaphore(n)) for n in names]

        w1_all = sb("w1_all", [P, NE + 1, 2 * INTER])
        w2_all = sb("w2_all", [P, NE + 1, 2 * D1])
        b1_all = sb("b1_all", [P, NE + 1, 2])
        b2_all = sb("b2_all", [NE + 1, D1])
        ident = sb("ident", [P, P])
        rec_all = sb("rec_all", [LQ, B, REC])
        mask_all = sb("mask_all", [LQ, B, NE], BF16)
        slots_all = sb("slots_all", [LQ, B, TOP])
        gates_all = sb("gates_all", [LQ, B, NE + 1])
        gate_k = sb("gate_k", [LQ, B, TOP])
        table = sb("table", [1, ROUTED_TILES, 2], I32)
        iota_e = sb("iota_e", [LQ, NE])
        shift = sb("shift", [P, NE])
        pad_row = sb("pad_row", [1, NE], I32)
        zero_rows = sb("zero_rows", [P, D1])
        bank = [stack.enter_context(nc.psum_tensor(f"bank{i}", [P, 512], F32)) for i in range(8)]
        rec4 = rec_all[:, :, :].rearrange("p (q s) n -> p s q n", s=SLOTS)
        mask4 = mask_all[:, :, :].rearrange("p (q s) n -> p s q n", s=SLOTS)
        slots4 = slots_all[:, :, :].rearrange("p (q s) n -> p s q n", s=SLOTS)
        w1_all4 = w1_all[:, :, :].rearrange("p (q s) n -> p s q n", s=SLOTS)
        w2_all4 = w2_all[:, :, :].rearrange("p (q s) n -> p s q n", s=SLOTS)

        weights_in, expert_in, made, small_in = sems("weights_in", "expert_in", "made", "small_in")
        x_in = sems(*[f"x_in{s}" for s in range(SLOTS)])
        xr_in = sems(*[f"xr_in{s}" for s in range(SLOTS)])
        c_in = sems("c_in0", "c_in1")
        h_out = sems(*[f"h_out{s}" for s in range(SLOTS)])
        base_out = sems(*[f"base_out{s}" for s in range(SLOTS)])
        scattered = sems(*[f"scattered{s}" for s in range(SLOTS)])
        (cols_ready, aug_ready, folds_made, folds_ready, ctx_stat6, ctx_stats, ctx_var, ctx_rstd, ctx_norm,
         x_stat6, x_stats, x_var, x_rstd, x_norm) = sems(
            "cols_ready", "aug_ready", "folds_made", "folds_ready", "ctx_stat6", "ctx_stats", "ctx_var", "ctx_rstd",
            "ctx_norm", "x_stat6", "x_stats", "x_var", "x_rstd", "x_norm")
        (ctx_transposed, ctx_t_copied, x_transposed, x_t_copied, q_made, q_copied, scores_made, rowmax_made,
         probs_made, rinv_made, probs_transposed, probs_t_copied, mix_made, mix_copied, attn_made,
         resid_made, resid_stat6, resid_stats, resid_var, resid_rstd, h_made, base_made) = sems(
            "ctx_transposed", "ctx_t_copied", "x_transposed", "x_t_copied", "q_made", "q_copied", "scores_made",
            "rowmax_made", "probs_made", "rinv_made", "probs_transposed", "probs_t_copied", "mix_made",
            "mix_copied", "attn_made", "resid_made", "resid_stat6", "resid_stats", "resid_var", "resid_rstd",
            "h_made", "base_made")
        (h_transposed, h_t_copied, logits_made, logit_sum, top_vals, top_idx, idx_float, picks_made, mask_made,
         msum_made, saved, rank_made, slot_sum, slot_picks, slots_made, slots_saved) = sems(
            "h_transposed", "h_t_copied", "logits_made", "logit_sum", "top_vals", "top_idx", "idx_float",
            "picks_made", "mask_made", "msum_made", "saved", "rank_made", "slot_sum", "slot_picks", "slots_made",
            "slots_saved")
        counts_made, dve_chain, shifted, gate_exps, pads_ready, pads_out, table_made, table_out, table_in = sems(
            "counts_made", "dve_chain", "shifted", "gate_exps", "pads_ready", "pads_out", "table_made", "table_out",
            "table_in")

        with ExitStack() as st1:
            def s1(name, shape, dt=F32):
                return sb(name, shape, dt, st1)

            wq_s, wqt_s, wo_s, wk_s, wv_s, bo_s, wk_aug, wv_aug = (
                w2_all[:, NE - 7 + k, :].rearrange("p (c n) -> p c n", c=2) for k in range(8))
            wk0, wk1, wv0, wv1 = wk_s[:, 0, :], wk_s[0:D2B, 1, :], wv_s[:, 0, :], wv_s[0:D2B, 1, :]
            bo_row = bo_s[0:D2C, 0, :]
            wk_aug, wv_aug = wk_aug[:, :, 0:D2 + 1], wv_aug[:, :, 0:D2 + 1]
            g1_s, b1_s, bq_s, bk_s, bv_s = (s1(n, [P, 2]) for n in ("g1_s", "b1_s", "bq_s", "bk_s", "bv_s"))
            g2_0, g2_1, b2_0, b2_1 = (s1("g2_0", [P, 1]), s1("g2_1", [D2C, 1]), s1("b2_0", [P, 1]),
                                      s1("b2_1", [D2B, 1]))
            uq = s1("uq", [P, 2])
            fold_q = s1("fold_q", [P, 2, D2 + 1])
            fold_o0, fold_o1 = s1("fold_o0", [P, D1]), s1("fold_o1", [D2C, D1])
            qs0, qs1 = s1("qs0", [P, 2]), s1("qs1", [D2C, 2])
            wr_s = s1("wr_s", [P, 2, NE])
            br_s = s1("br_s", [LQ, NE])
            tri, ones = s1("tri", [LQ, LQ], BF16), s1("ones", [LQ, P], BF16)
            iota_slot = s1("iota_slot", [P, NE])
            tile_no = s1("tile_no", [P, 1])
            mhalf = s1("mhalf", [P, 4])
            c_sb = [s1(f"c_sb{i}", [P, 3, D2]) for i in range(2)]
            z = [s1(f"z{i}", [P, 3, D2 + 1]) for i in range(SLOTS)]
            x_sb = [s1(f"x_sb{i}", [LQ, D1]) for i in range(SLOTS)]
            xr_sb = [s1(f"xr_sb{i}", [LQ, D1]) for i in range(SLOTS)]
            h_sb = [s1(f"h_sb{i}", [LQ, D1]) for i in range(SLOTS)]

            def two(name, shape, dt=F32):
                return [s1(f"{name}{i}", shape, dt) for i in range(2)]

            c6, cmv, crs = two("c6", [P, 3, 6]), two("cmv", [P, 3, 2]), two("crs", [P, 2, 3])
            x6, xmv, xrs = two("x6", [LQ, 6]), two("xmv", [LQ, 2]), two("xrs", [LQ, 2])
            r6, rmv, rrs = two("r6", [LQ, 6]), two("rmv", [LQ, 2]), two("rrs", [LQ, 2])
            z1, z1t = two("z1", [LQ, D1]), two("z1t", [P, 2 * LQ])
            qt0, qt1 = two("qt0", [P, LQ]), two("qt1", [D2C, LQ])
            zt0, zt1 = two("zt0", [P, LK]), two("zt1", [D2C, LK])
            probs, probs_t = two("probs", [LQ, LK]), two("probs_t", [P, 3, LQ])
            negmax, rowsum, rinv = two("negmax", [LQ, 1]), two("rowsum", [LQ, 1]), two("rinv", [LQ, 1])
            mix0, mix1 = two("mix0", [P, LQ]), two("mix1", [D2C, LQ])
            resid, base_sb, h_t = two("resid", [LQ, D1]), two("base_sb", [LQ, D1]), two("h_t", [P, 2 * LQ])
            rec, idx8 = two("rec", [LQ, REC]), two("idx8", [LQ, 8], U32)
            picks, mask, msum = two("picks", [LQ, TOP, NE]), two("mask", [LQ, NE], BF16), two("msum", [LQ, NE], BF16)
            slotf, slotp, slot = two("slotf", [LQ, NE]), two("slotp", [LQ, TOP, NE]), two("slot", [LQ, TOP], I32)
            cnt_i, cnt_s = s1("cnt_i", [P, NE], I32), s1("cnt_s", [P, NE], I32)
            ntile, cum, below, unit = (s1(n, [P, NE]) for n in ("ntile", "cum", "below", "unit"))
            tcol = s1("tcol", [P, 8])
            tab_s = s1("tab_s", [P, 2], I32)
            gsum = s1("gsum", [LQ, B])
            MADE = 16

            zt_ps0, zt_ps1 = bank[2], bank[3]
            probs_ps = bank[4]
            mix_ps, attn_ps = bank[5][:, 0:2 * LQ], bank[5][0:LQ, 256:512]
            z1_ps, q_ps = bank[6][:, 0:2 * LQ], bank[6][:, 256:256 + 2 * LQ]
            h_ps, logit_ps, rank_ps = bank[7][:, 0:2 * LQ], bank[7][0:LQ, 256:256 + NE], bank[7][0:LQ, 320:320 + NE]

            def inside(b):
                return not b.fixed or 0 <= b.r < B

            def rows(v4, b):
                return v4[b.slot(SLOTS), bass.ds(b.turn(SLOTS), 1)].rearrange("o p n -> (o p) n")

            block = st1.enter_context(nc.Block())

            @block.sync
            def _(sp):
                for dst, src in (
                    (wq_s[:, :, :], wq.rearrange("(c p) e -> p c e", p=P)), (wqt_s[:, :, :], wqt.rearrange("(c p) e -> p c e", p=P)),
                    (wk0[:, :], wk[0:P, :]), (wk1[:, :], wk[P:D2, :]), (wv0[:, :], wv[0:P, :]), (wv1[:, :], wv[P:D2, :]),
                    (wk_aug[:, :, 0:D2], wkt.rearrange("(c p) e -> p c e", p=P)),
                    (wv_aug[:, :, 0:D2], wvt.rearrange("(c p) e -> p c e", p=P)),
                    (wo_s[:, :, :], wo.rearrange("(c p) e -> p c e", p=P)), (bo_row[D2B:D2C, :], bo),
                    (g1_s[:, :], g1c), (b1_s[:, :], b1c), (bq_s[:, :], bqc), (bk_s[:, :], bkc), (bv_s[:, :], bvc),
                    (g2_0[:, :], g2c[0:P, :]), (g2_1[0:D2B, :], g2c[P:D2, :]),
                    (b2_0[:, :], b2c[0:P, :]), (b2_1[:, :], b2c[P:D2, :]),
                ):
                    sp.dma_start(dst, src).then_inc(weights_in, 16)

                def load_x(b):
                    if b.has(SLOTS):
                        sp.wait_ge(x_norm, b.count(1 - SLOTS))
                    sp.dma_start(x_sb[b.slot(SLOTS)][:, :], rows(x4, b)).then_inc(x_in[b.slot(SLOTS)], 16)

                def load_ctx(b):
                    if b.has(2):
                        sp.wait_ge(ctx_norm, b.count(-1))
                    src = rows(c4, b)
                    s = b.slot(2)
                    sp.dma_start(c_sb[s][:, 0:2, :], src[0:2 * P, :].rearrange("(t p) d -> p t d", p=P)).then_inc(c_in[s], 16)
                    sp.dma_start(c_sb[s][0:KT[2], 2, :], src[2 * P:LK, :]).then_inc(c_in[s], 16)

                def load_resid(b):
                    if b.has(SLOTS):
                        sp.wait_ge(resid_made, b.count(1 - SLOTS))
                        alone(sp)
                    sp.dma_start(xr_sb[b.slot(SLOTS)][:, :], rows(x4, b)).then_inc(xr_in[b.slot(SLOTS)], 16)

                sp.wait_ge(made, MADE)
                for b in range(3):
                    load_x(At(0, b, UN))
                load_ctx(At(0, 0, UN))

                def step(i):
                    b = i.back(-4)
                    if inside(b):
                        load_x(b)
                    b = i.back(-2)
                    if inside(b):
                        load_ctx(b)
                    b = i.back(-1)
                    if inside(b):
                        load_resid(b)
                        s = b.slot(SLOTS)
                        sp.dma_start(w1_all4[:, s, bass.ds(b.turn(SLOTS), 1), :].rearrange("p o n -> p (o n)"),
                                     rows(w1_4, b)).then_inc(expert_in, 16)
                        sp.dma_start(w2_all4[:, s, bass.ds(b.turn(SLOTS), 1), :].rearrange("p o n -> p (o n)"),
                                     rows(w2_4, b)).then_inc(expert_in, 16)
                    b = i.back(3)
                    if inside(b):
                        sp.wait_ge(h_made, b.count(1))
                        sp.dma_start(rows(h4, b), h_sb[b.slot(SLOTS)][:, :]).then_inc(h_out[b.slot(SLOTS)], 16)
                        sp.wait_ge(base_made, b.count(1))
                        sp.dma_start(rows(base4, b), base_sb[b.slot(2)][:, :]).then_inc(base_out[b.slot(SLOTS)], 16)

                walk(sp, step, -1, B + 3, UN, head=8, tail=7)

                sp.wait_ge(pads_ready, 1)
                with sp.Fori(0, NE) as e:
                    row = sp.value_load(pad_row[0:1, bass.ds(e, 1)], min_val=TOKENS, max_val=LIST_END - P)
                    sp.dma_start(xs[bass.ds(row, P), :], zero_rows[:, :]).then_inc(pads_out, 16)
                sp.wait_ge(table_made, 1)
                sp.dma_start(tab_d, tab_s[0:ROUTED_TILES, :]).then_inc(table_out, 16)
                sp.wait_ge(table_out, 16)
                sp.dma_start(table[0:1, :, :], tab_d.rearrange("(o t) n -> o t n", o=1)).then_inc(table_in, 16)

            @block.gpsimd
            def _(pool):
                n = [0]

                def const(ins):
                    n[0] += 1
                    ins.then_inc(made, 1)
                    return n[0]

                const(pool.memset(mhalf[:, :], -0.5))
                for s in range(2):
                    const(pool.memset(c_sb[s][:, :, :], 0.0))
                for s in range(SLOTS):
                    const(pool.memset(z[s][:, :, D2:D2 + 1], 1.0))
                const(pool.memset(msum[0][:, :], 0.0))
                const(pool.memset(ones[:, :], 1.0))
                const(pool.iota(iota_e[:, :], pattern=[[1, NE]], base=0, channel_multiplier=0,
                                allow_small_or_imprecise_dtypes=True))
                const(pool.iota(iota_slot[:, :], pattern=[[CAP, NE]], base=TOKENS, channel_multiplier=0,
                                allow_small_or_imprecise_dtypes=True))
                const(pool.iota(tile_no[:, :], pattern=[[0, 1]], base=0, channel_multiplier=1,
                                allow_small_or_imprecise_dtypes=True))
                const(pool.memset(ident[:, :], 0.0))
                k = const(pool.memset(tri[:, :], 1.0))
                pool.wait_ge(made, k)
                const(pool.affine_select(out=ident[:, :], in_=ident[:, :], compare_op=ALU.not_equal, fill=1.0,
                                         base=0, pattern=[[-1, P]], channel_multiplier=1))
                k = const(pool.affine_select(out=tri[:, :], in_=tri[:, :], compare_op=ALU.is_gt, fill=0.0,
                                             base=0, pattern=[[1, LQ]], channel_multiplier=-1))
                assert k == MADE, k
                pool.dma_start(wr_s[:, :, :], wr.rearrange("(c p) e -> p c e", p=P)).then_inc(small_in, 16)
                pool.dma_start(br_s[:, :], br.partition_broadcast(LQ)).then_inc(small_in, 16)
                pool.dma_start(b1_all[:, :, :], be1).then_inc(small_in, 16)
                pool.dma_start(b2_all[:, :], b2).then_inc(small_in, 16)

                pool.wait_ge(made, MADE)

                def step(i):
                    b = i.back(-1)
                    if inside(b):
                        s = b.slot(2)
                        pool.wait_ge(ctx_stats, b.count(1))
                        alone(pool)
                        pool.tensor_scalar(crs[s][:, 0, :], cmv[s][:, :, 1], EPS, None, ALU.add).then_inc(ctx_var, 1)
                        pool.wait_ge(x_stats, b.count(1))
                        alone(pool)
                        pool.tensor_scalar(xrs[s][:, 0:1], xmv[s][:, 1:2], 1.0 + EPS, EPS * EPS, ALU.mult,
                                           ALU.add).then_inc(x_var, 1)
                        pool.wait_ge(ctx_var, b.count(1))
                        pool.tensor_tensor(crs[s][:, 1, :], crs[s][:, 0, :], mhalf[:, 0:3], ALU.pow).then_inc(ctx_rstd, 1)
                        pool.wait_ge(x_var, b.count(1))
                        pool.tensor_tensor(xrs[s][:, 1:2], xrs[s][:, 0:1], mhalf[0:LQ, 0:1], ALU.pow).then_inc(x_rstd, 1)
                    b = i.back(3)
                    if inside(b):
                        s, s4 = b.slot(2), b.slot(SLOTS)
                        pool.wait_ge(mask_made, b.count(1))
                        if b.has(1):
                            pool.wait_ge(rank_made, b.count(0))
                            pool.wait_ge(msum_made, b.count(0))
                        pool.tensor_tensor(msum[1 - s][:, :], msum[s][:, :], mask[s][:, :], ALU.add).then_inc(msum_made, 1)
                        pool.tensor_copy(mask4[:, s4, bass.ds(b.turn(SLOTS), 1), :].rearrange("p o n -> p (o n)"),
                                         mask[s][:, :])
                        pool.tensor_copy(rec4[:, s4, bass.ds(b.turn(SLOTS), 1), :].rearrange("p o n -> p (o n)"),
                                         rec[s][:, :]).then_inc(saved, 1)
                    b = i.back(2)
                    if inside(b):
                        s = b.slot(2)
                        pool.wait_ge(resid_stats, b.count(1))
                        alone(pool)
                        pool.tensor_scalar(rrs[s][:, 0:1], rmv[s][:, 1:2], EPS, None, ALU.add).then_inc(resid_var, 1)
                        pool.wait_ge(resid_var, b.count(1))
                        pool.tensor_tensor(rrs[s][:, 1:2], rrs[s][:, 0:1], mhalf[0:LQ, 0:1], ALU.pow).then_inc(resid_rstd, 1)
                    b = i.back(3)
                    if inside(b):
                        s, s4 = b.slot(2), b.slot(SLOTS)
                        pool.wait_ge(slots_made, b.count(1))
                        pool.tensor_copy(slots4[:, s4, bass.ds(b.turn(SLOTS), 1), :].rearrange("p o n -> p (o n)"),
                                         slot[s][:, :]).then_inc(slots_saved, 1)
                        if b.has(SLOTS):
                            pool.wait_ge(scattered[s4], b.turn(SLOTS) * (16 * TOP))
                            alone(pool)
                        for k in range(TOP):
                            pool.indirect_dma_start(xs, bass.IndirectOffsetOnAxis(ap=slot[s][:, k:k + 1], axis=0),
                                                    h_sb[s4][:, :], None).then_inc(scattered[s4], 16)
                    b = i.back(2)
                    if inside(b):
                        s = b.slot(2)
                        pool.wait_ge(h_made, b.count(1))
                        if b.has(2):
                            o = b.back(2)
                            pool.wait_ge(base_out[o.slot(SLOTS)], o.turn(SLOTS, 1) * 16)
                        pool.tensor_tensor(base_sb[s][:, :], resid[s][:, :], h_sb[b.slot(SLOTS)][:, :],
                                           ALU.add).then_inc(base_made, 1)

                walk(pool, step, -1, B + 3, UN, head=8, tail=4)

            @block.scalar
            def _(act):
                act.wait_ge(folds_ready, 1)

                def step(i):
                    b = i
                    if inside(b):
                        s = b.slot(2)
                        act.wait_ge(ctx_transposed, b.count(1))
                        if b.has(2):
                            act.wait_ge(scores_made, b.count(-1))
                        act.activation(zt0[s][:, :], zt_ps0[:, 0:LK], ACT.Copy)
                        act.activation(zt1[s][:, :], zt_ps1[0:D2C, 0:LK], ACT.Copy).then_inc(ctx_t_copied, 1)
                        act.wait_ge(x_transposed, b.count(1))
                        if b.has(2):
                            act.wait_ge(q_made, b.count(-1))
                        act.activation(z1t[s][:, :], z1_ps, ACT.Copy).then_inc(x_t_copied, 1)
                    b = i.back(2)
                    if inside(b):
                        s = b.slot(2)
                        act.wait_ge(probs_transposed, b.count(1))
                        if b.has(2):
                            act.wait_ge(mix_made, b.count(-1))
                        act.activation(probs_t[s][:, 0:2, :], probs_ps[:, 0:2 * LQ].rearrange("p (t q) -> p t q", q=LQ), ACT.Copy)
                        act.activation(probs_t[s][0:KT[2], 2, :], probs_ps[0:KT[2], 2 * LQ:3 * LQ],
                                       ACT.Copy).then_inc(probs_t_copied, 1)
                    b = i.back(1)
                    if inside(b):
                        s = b.slot(2)
                        act.wait_ge(rowmax_made, b.count(1))
                        if b.has(2):
                            act.wait_ge(probs_transposed, b.count(-1))
                            act.wait_ge(rinv_made, b.count(-1))
                        act.activation(probs[s][:, :], bank[s][0:LQ, 0:LK], ACT.Exp, bias=negmax[s][:, 0:1],
                                       accum_out=rowsum[s][:, 0:1]).then_inc(probs_made, 1)
                    b = i
                    if inside(b):
                        s = b.slot(2)
                        act.wait_ge(q_made, b.count(1))
                        if b.has(2):
                            act.wait_ge(scores_made, b.count(-1))
                        act.activation(qt0[s][:, :], q_ps[:, 0:LQ], ACT.Identity, bias=qs0[:, 1:2], scale=qs0[:, 0:1])
                        act.activation(qt1[s][:, :], q_ps[0:D2C, LQ:2 * LQ], ACT.Identity, bias=qs1[:, 1:2],
                                       scale=qs1[:, 0:1]).then_inc(q_copied, 1)
                    b = i.back(3)
                    if inside(b):
                        s = b.slot(2)
                        act.wait_ge(h_transposed, b.count(1))
                        if b.has(2):
                            act.wait_ge(logits_made, b.count(-1))
                        act.activation(h_t[s][:, :], h_ps, ACT.Copy).then_inc(h_t_copied, 1)
                    b = i.back(2)
                    if inside(b):
                        s = b.slot(2)
                        act.wait_ge(mix_made, b.count(1))
                        if b.has(2):
                            act.wait_ge(attn_made, b.count(-1))
                        act.activation(mix0[s][:, :], mix_ps[:, 0:LQ], ACT.Copy)
                        act.activation(mix1[s][:, :], mix_ps[0:D2C, LQ:2 * LQ], ACT.Copy).then_inc(mix_copied, 1)

                walk(act, step, -1, B + 3, UN, head=8, tail=4)
                act.wait_ge(shifted, 1)
                act.activation(gates_all[:, :, 0:NE], gates_all[:, :, 0:NE], ACT.Exp).then_inc(gate_exps, 1)
                act.activation(gate_k[:, :, :], gate_k[:, :, :], ACT.Exp).then_inc(gate_exps, 1)

            @block.vector
            def _(dve):
                dve.memset(g2_1[D2B:D2C, :], 1.0).then_inc(dve_chain, 1)
                dve.memset(unit[:, :], 1.0).then_inc(dve_chain, 1)
                dve.memset(zero_rows[:, :], 0.0).then_inc(dve_chain, 1)
                dve.memset(gates_all[:, :, NE:NE + 1], 1.0).then_inc(dve_chain, 1)
                dve.wait_ge(weights_in, 16 * 19)
                dve.wait_ge(cols_ready, 1)
                dve.tensor_tensor(wk_aug[:, :, D2], bank[0][:, 0:2], bk_s[:, :], ALU.add)
                dve.tensor_tensor(wv_aug[:, :, D2], bank[0][:, 2:4], bv_s[:, :], ALU.add)
                dve.tensor_tensor(uq[:, :], bank[0][:, 4:6], bq_s[:, :], ALU.add).then_inc(aug_ready, 1)
                dve.wait_ge(folds_made, 1)
                dve.wait_ge(dve_chain, 4)
                for a in range(2):
                    dve.tensor_scalar(fold_q[:, a, :], bank[1][:, a * 256:a * 256 + D2 + 1], g1_s[:, a:a + 1], None, ALU.mult)
                dve.tensor_scalar(qs0[:, 0:1], g2_0[:, :], SCALE, None, ALU.mult)
                dve.tensor_scalar(qs1[:, 0:1], g2_1[:, :], SCALE, None, ALU.mult)
                dve.tensor_scalar(fold_o0[:, :], bank[2][:, 0:D1], g2_0[:, :], None, ALU.mult)
                dve.tensor_scalar(fold_o1[:, :], bank[2][0:D2C, D1:2 * D1], g2_1[:, :], None, ALU.mult).then_inc(dve_chain, 1)
                dve.wait_ge(dve_chain, 5)
                dve.tensor_tensor(qs0[:, 1:2], bank[3][:, 0:1], qs0[:, 0:1], ALU.mult)
                dve.tensor_tensor(qs1[:, 1:2], bank[3][0:D2C, 1:2], qs1[:, 0:1], ALU.mult)
                dve.tensor_tensor(fold_o1[D2B:D2C, :], fold_o1[D2B:D2C, :], bo_row[D2B:D2C, :], ALU.add).then_inc(folds_ready, 1)
                dve.wait_ge(made, MADE)
                dve.wait_ge(small_in, 64)

                def step(i):
                    b = i.back(-1)
                    if inside(b):
                        s, s4 = b.slot(2), b.slot(SLOTS)
                        dve.wait_ge(c_in[s], b.turn(2, 1) * 32)
                        for t in range(3):
                            ins = dve.bn_stats(c6[s][:, t, :], c_sb[s][:, t, :])
                        ins.then_inc(ctx_stat6, 1)
                        dve.wait_ge(x_in[s4], b.turn(SLOTS, 1) * 16)
                        dve.bn_stats(x6[s][:, :], x_sb[s4][:, :]).then_inc(x_stat6, 1)
                        dve.wait_ge(ctx_stat6, b.count(1))
                        alone(dve)
                        for t in range(3):
                            ins = dve.bn_aggr(cmv[s][:, t, :], c6[s][:, t, :])
                        ins.then_inc(ctx_stats, 1)
                        dve.wait_ge(x_stat6, b.count(1))
                        alone(dve)
                        dve.bn_aggr(xmv[s][:, :], x6[s][:, :]).then_inc(x_stats, 1)
                    b = i.back(1)
                    if inside(b):
                        s = b.slot(2)
                        dve.wait_ge(scores_made, b.count(1))
                        dve.tensor_reduce(negmax[s][:, :], bank[s][0:LQ, 0:LK], AX.X, ALU.max, negate=True)\
                           .then_inc(rowmax_made, 1)
                    b = i.back(-1)
                    if inside(b):
                        s, s4 = b.slot(2), b.slot(SLOTS)
                        dve.wait_ge(ctx_rstd, b.count(1))
                        if b.has(SLOTS):
                            dve.wait_ge(mix_made, b.count(1 - SLOTS))
                        for t in range(3):
                            ins = dve.tensor_scalar(z[s4][:, t, 0:D2], c_sb[s][:, t, :], cmv[s][:, t, 0:1],
                                                    crs[s][:, 1, t:t + 1], ALU.subtract, ALU.mult)
                        ins.then_inc(ctx_norm, 1)
                        dve.wait_ge(x_rstd, b.count(1))
                        if b.has(2):
                            dve.wait_ge(x_transposed, b.count(-1))
                        dve.tensor_scalar(z1[s][:, :], x_sb[s4][:, :], xmv[s][:, 0:1], xrs[s][:, 1:2], ALU.subtract,
                                          ALU.mult).then_inc(x_norm, 1)
                    b = i.back(3)
                    if inside(b):
                        s = b.slot(2)
                        dve.wait_ge(logits_made, b.count(1))
                        if b.has(2):
                            dve.wait_ge(saved, b.count(-1))
                        dve.tensor_tensor(rec[s][:, 0:NE], logit_ps, br_s[:, :], ALU.add).then_inc(logit_sum, 1)
                        dve.wait_ge(logit_sum, b.count(1))
                        alone(dve)
                        dve.max(rec[s][:, NE:NE + 8], rec[s][:, 0:NE]).then_inc(top_vals, 1)
                        dve.wait_ge(top_vals, b.count(1))
                        alone(dve)
                        dve.max_index(idx8[s][:, :], rec[s][:, NE:NE + 8], rec[s][:, 0:NE]).then_inc(top_idx, 1)
                        dve.wait_ge(top_idx, b.count(1))
                        dve.tensor_copy(rec[s][:, NE + 8:REC], idx8[s][:, 0:TOP]).then_inc(idx_float, 1)
                        dve.wait_ge(idx_float, b.count(1))
                        dve.tensor_tensor(picks[s][:, :, :], iota_e[:, :].unsqueeze(1).to_broadcast([LQ, TOP, NE]),
                                          rec[s][:, NE + 8:REC].unsqueeze(2).to_broadcast([LQ, TOP, NE]),
                                          ALU.is_equal).then_inc(picks_made, 1)
                        dve.wait_ge(picks_made, b.count(1))
                        with nc.allow_low_precision(reason="zeros and ones"):
                            dve.tensor_reduce(mask[s][:, :], picks[s][:, :, :].rearrange("p k e -> p e k"), AX.X,
                                              ALU.add).then_inc(mask_made, 1)
                    b = i.back(2)
                    if inside(b):
                        s, s4 = b.slot(2), b.slot(SLOTS)
                        dve.wait_ge(probs_made, b.count(1))
                        dve.reciprocal(rinv[s][:, :], rowsum[s][:, :]).then_inc(rinv_made, 1)
                        dve.wait_ge(rinv_made, b.count(1))
                        dve.wait_ge(attn_made, b.count(1))
                        dve.wait_ge(xr_in[s4], b.turn(SLOTS, 1) * 16)
                        if b.has(2):
                            dve.wait_ge(base_made, b.count(-1))
                        dve.scalar_tensor_tensor(resid[s][:, :], attn_ps, rinv[s][:, 0:1], xr_sb[s4][:, :], ALU.mult,
                                                 ALU.add).then_inc(resid_made, 1)
                        dve.wait_ge(resid_made, b.count(1))
                        dve.bn_stats(r6[s][:, :], resid[s][:, :]).then_inc(resid_stat6, 1)
                        dve.wait_ge(resid_stat6, b.count(1))
                        alone(dve)
                        dve.bn_aggr(rmv[s][:, :], r6[s][:, :]).then_inc(resid_stats, 1)
                    b = i.back(3)
                    if inside(b):
                        s = b.slot(2)
                        dve.wait_ge(rank_made, b.count(1))
                        dve.tensor_tensor(slotf[s][:, :], rank_ps, iota_slot[0:LQ, :], ALU.add).then_inc(slot_sum, 1)
                        dve.wait_ge(slot_sum, b.count(1))
                        dve.tensor_tensor(slotp[s][:, :, :], picks[s][:, :, :],
                                          slotf[s][:, :].unsqueeze(1).to_broadcast([LQ, TOP, NE]),
                                          ALU.mult).then_inc(slot_picks, 1)
                        dve.wait_ge(slot_picks, b.count(1))
                        if b.has(2):
                            o = b.back(2)
                            dve.wait_ge(scattered[o.slot(SLOTS)], o.turn(SLOTS, 1) * (16 * TOP))
                            dve.wait_ge(slots_saved, b.count(-1))
                        with nc.allow_low_precision(reason="row numbers, exact in float32"):
                            dve.tensor_reduce(slot[s][:, :], slotp[s][:, :, :], AX.X, ALU.add).then_inc(slots_made, 1)
                    b = i.back(2)
                    if inside(b):
                        s, s4 = b.slot(2), b.slot(SLOTS)
                        dve.wait_ge(resid_rstd, b.count(1))
                        if b.has(SLOTS):
                            o = b.back(SLOTS)
                            dve.wait_ge(h_out[s4], o.turn(SLOTS, 1) * 16)
                            dve.wait_ge(scattered[s4], o.turn(SLOTS, 1) * (16 * TOP))
                            dve.wait_ge(h_transposed, o.count(1))
                        dve.tensor_scalar(h_sb[s4][:, :], resid[s][:, :], rmv[s][:, 0:1], rrs[s][:, 1:2], ALU.subtract,
                                          ALU.mult).then_inc(h_made, 1)

                walk(dve, step, -1, B + 3, UN, head=8, tail=4)

                at = [5]

                def chain(ins):
                    at[0] += 1
                    ins.then_inc(dve_chain, 1)
                    dve.wait_ge(dve_chain, at[0])

                dve.wait_ge(saved, B)
                top = rec_all[:, :, NE:NE + 1]
                dve.tensor_tensor(gates_all[:, :, 0:NE], rec_all[:, :, 0:NE], top.to_broadcast([LQ, B, NE]), ALU.subtract)
                dve.tensor_tensor(gate_k[:, :, :], rec_all[:, :, NE:NE + TOP], top.to_broadcast([LQ, B, TOP]),
                                  ALU.subtract).then_inc(shifted, 1)
                dve.wait_ge(counts_made, 1)
                counts = bank[0][:, 0:NE]
                chain(dve.tensor_scalar(cnt_i[:, :], counts, float(P - 1), None, ALU.add))
                dve.tensor_tensor(pad_row[0:1, :], counts[0:1, :], iota_slot[0:1, :], ALU.add).then_inc(pads_ready, 1)
                chain(dve.tensor_scalar(cnt_s[:, :], cnt_i[:, :], P.bit_length() - 1, None, ALU.arith_shift_right))
                chain(dve.tensor_copy(ntile[:, :], cnt_s[:, :]))
                chain(dve.tensor_tensor_scan(cum[:, :], unit[:, :], ntile[:, :], 0.0, ALU.mult, ALU.add))
                chain(dve.tensor_scalar(below[:, :], cum[:, :], tile_no[:, :], None, ALU.is_le))
                expert, before, real, own, e2, r0, r1 = (tcol[:, k:k + 1] for k in range(7))
                chain(dve.tensor_reduce(expert, below[:, :], AX.X, ALU.add))
                chain(dve.tensor_tensor(below[:, :], below[:, :], ntile[:, :], ALU.mult))
                chain(dve.tensor_reduce(before, below[:, :], AX.X, ALU.add))
                chain(dve.tensor_scalar(real, expert, float(NE), None, ALU.is_lt))
                chain(dve.tensor_tensor(own, tile_no[:, :], before, ALU.subtract))
                chain(dve.tensor_tensor(e2, expert, real, ALU.mult))
                chain(dve.tensor_tensor(own, own, real, ALU.mult))
                chain(dve.tensor_scalar(r0, e2, float(CAP), float(TOKENS), ALU.mult, ALU.add))
                chain(dve.tensor_scalar(r1, own, float(P), None, ALU.mult))
                dve.tensor_copy(tab_s[:, 0:1], e2)
                dve.tensor_tensor(tab_s[:, 1:2], r0, r1, ALU.add).then_inc(table_made, 1)
                chain(dve.tensor_tensor(cum[:, :], cum[:, :], ntile[:, :], ALU.subtract))
                chain(dve.tensor_scalar(cum[:, :], cum[:, :], float(P), float(TOKENS), ALU.mult, ALU.add))
                chain(dve.tensor_tensor(shift[:, :], cum[:, :], iota_slot[:, :], ALU.subtract))
                dve.wait_ge(gate_exps, 2)
                chain(dve.tensor_reduce(gsum[:, :], gates_all[:, :, 0:NE], AX.X, ALU.add))
                chain(dve.reciprocal(gsum[:, :], gsum[:, :]))
                chain(dve.tensor_tensor(gates_all[:, :, 0:NE], gates_all[:, :, 0:NE], mask_all[:, :, :], ALU.mult))
                chain(dve.tensor_tensor(gates_all[:, :, 0:NE], gates_all[:, :, 0:NE],
                                        gsum[:, :].unsqueeze(2).to_broadcast([LQ, B, NE]), ALU.mult))
                chain(dve.tensor_tensor(gate_k[:, :, :], gate_k[:, :, :],
                                        gsum[:, :].unsqueeze(2).to_broadcast([LQ, B, TOP]), ALU.mult))

            @block.tensor
            def _(pe):
                pe.wait_ge(weights_in, 16 * 19)
                for m in range(2):
                    cut = slice(m * P, m * P + P)
                    pe.matmul(bank[0][:, m:m + 1], wk0[:, cut], b2_0[:, :], start=True, stop=False)
                    pe.matmul(bank[0][:, m:m + 1], wk1[:, cut], b2_1[:, :], start=False, stop=True)
                    pe.matmul(bank[0][:, 2 + m:3 + m], wv0[:, cut], b2_0[:, :], start=True, stop=False)
                    pe.matmul(bank[0][:, 2 + m:3 + m], wv1[:, cut], b2_1[:, :], start=False, stop=True)
                    pe.matmul(bank[0][:, 4 + m:5 + m], wq_s[:, 0, cut], b1_s[:, 0:1], start=True, stop=False)
                    mm = pe.matmul(bank[0][:, 4 + m:5 + m], wq_s[:, 1, cut], b1_s[:, 1:2], start=False, stop=True)
                mm.then_inc(cols_ready, 1)
                pe.wait_ge(aug_ready, 1)
                for a in range(2):
                    for c in range(2):
                        pe.matmul(bank[1][:, a * 256:a * 256 + D2 + 1], wqt_s[:, c, a * P:a * P + P], wk_aug[:, c, :],
                                  start=(c == 0), stop=(c == 1))
                for c in range(2):
                    pe.matmul(bank[2][:, 0:D1], wv_aug[:, c, 0:P], wo_s[:, c, :], start=(c == 0), stop=(c == 1))
                for c in range(2):
                    pe.matmul(bank[2][0:D2C, D1:2 * D1], wv_aug[:, c, P:D2 + 1], wo_s[:, c, :], start=(c == 0), stop=(c == 1))
                for c in range(2):
                    pe.matmul(bank[3][:, 0:1], wk_aug[:, c, 0:P], uq[:, c:c + 1], start=(c == 0), stop=(c == 1))
                for c in range(2):
                    mm = pe.matmul(bank[3][0:D2C, 1:2], wk_aug[:, c, P:D2 + 1], uq[:, c:c + 1], start=(c == 0), stop=(c == 1))
                mm.then_inc(folds_made, 1)
                pe.wait_ge(folds_ready, 1)
                pe.wait_ge(made, MADE)
                pe.wait_ge(small_in, 64)

                def step(i):
                    b = i
                    if inside(b):
                        s, s4 = b.slot(2), b.slot(SLOTS)
                        pe.wait_ge(ctx_norm, b.count(1))
                        pe.wait_ge(ctx_t_copied, b.count(0))
                        for t in range(3):
                            k = KT[t]
                            pe.transpose(zt_ps0[:, t * P:t * P + k], z[s4][0:k, t, 0:P], ident[0:k, 0:k])
                            mm = pe.transpose(zt_ps1[0:D2C, t * P:t * P + k], z[s4][0:k, t, P:D2 + 1], ident[0:k, 0:k])
                        mm.then_inc(ctx_transposed, 1)
                        pe.wait_ge(x_norm, b.count(1))
                        pe.wait_ge(q_copied, b.count(0))
                        for c in range(2):
                            mm = pe.transpose(z1_ps[:, c * LQ:(c + 1) * LQ], z1[s][:, c * P:c * P + P], ident[0:LQ, 0:LQ])
                        mm.then_inc(x_transposed, 1)
                    b = i.back(1)
                    if inside(b):
                        s = b.slot(2)
                        pe.wait_ge(ctx_t_copied, b.count(1))
                        pe.wait_ge(q_copied, b.count(1))
                        if b.has(2):
                            pe.wait_ge(probs_made, b.count(-1))
                        pe.matmul(bank[s][0:LQ, 0:LK], qt0[s][:, :], zt0[s][:, :], start=True, stop=False)
                        pe.matmul(bank[s][0:LQ, 0:LK], qt1[s][:, :], zt1[s][:, :], start=False, stop=True)\
                          .then_inc(scores_made, 1)
                    b = i.back(2)
                    if inside(b):
                        s = b.slot(2)
                        pe.wait_ge(probs_made, b.count(1))
                        pe.wait_ge(probs_t_copied, b.count(0))
                        for t in range(3):
                            k = KT[t]
                            mm = pe.transpose(probs_ps[0:k, t * LQ:(t + 1) * LQ], probs[s][:, t * P:t * P + k], ident[0:LQ, 0:LQ])
                        mm.then_inc(probs_transposed, 1)
                    b = i
                    if inside(b):
                        s = b.slot(2)
                        pe.wait_ge(x_t_copied, b.count(1))
                        for c in range(2):
                            pe.matmul(q_ps[:, 0:LQ], fold_q[:, c, 0:P], z1t[s][:, c * LQ:(c + 1) * LQ],
                                      start=(c == 0), stop=(c == 1))
                        for c in range(2):
                            mm = pe.matmul(q_ps[0:D2C, LQ:2 * LQ], fold_q[:, c, P:D2 + 1], z1t[s][:, c * LQ:(c + 1) * LQ],
                                           start=(c == 0), stop=(c == 1))
                        mm.then_inc(q_made, 1)
                    b = i.back(3)
                    if inside(b):
                        s, s4 = b.slot(2), b.slot(SLOTS)
                        pe.wait_ge(h_made, b.count(1))
                        pe.wait_ge(slot_sum, b.count(0))
                        for c in range(2):
                            mm = pe.transpose(h_ps[:, c * LQ:(c + 1) * LQ], h_sb[s4][:, c * P:c * P + P], ident[0:LQ, 0:LQ])
                        mm.then_inc(h_transposed, 1)
                    b = i.back(2)
                    if inside(b):
                        s, s4 = b.slot(2), b.slot(SLOTS)
                        pe.wait_ge(probs_t_copied, b.count(1))
                        pe.wait_ge(resid_made, b.count(0))
                        for t in range(3):
                            pe.matmul(mix_ps[:, 0:LQ], z[s4][0:KT[t], t, 0:P], probs_t[s][0:KT[t], t, :],
                                      start=(t == 0), stop=(t == 2))
                        for t in range(3):
                            mm = pe.matmul(mix_ps[0:D2C, LQ:2 * LQ], z[s4][0:KT[t], t, P:D2 + 1], probs_t[s][0:KT[t], t, :],
                                           start=(t == 0), stop=(t == 2))
                        mm.then_inc(mix_made, 1)
                    b = i.back(3)
                    if inside(b):
                        s = b.slot(2)
                        pe.wait_ge(h_t_copied, b.count(1))
                        for c in range(2):
                            mm = pe.matmul(logit_ps, h_t[s][:, c * LQ:(c + 1) * LQ], wr_s[:, c, :], start=(c == 0), stop=(c == 1))
                        mm.then_inc(logits_made, 1)
                    b = i.back(2)
                    if inside(b):
                        s = b.slot(2)
                        pe.wait_ge(mix_copied, b.count(1))
                        pe.matmul(attn_ps, mix0[s][:, :], fold_o0[:, :], start=True, stop=False)
                        pe.matmul(attn_ps, mix1[s][:, :], fold_o1[:, :], start=False, stop=True).then_inc(attn_made, 1)
                    b = i.back(3)
                    if inside(b):
                        s = b.slot(2)
                        pe.wait_ge(mask_made, b.count(1))
                        pe.wait_ge(msum_made, b.count(0))
                        pe.matmul(rank_ps, tri[:, :], mask[s][:, :], start=True, stop=False)
                        pe.matmul(rank_ps, ones[:, 0:LQ], msum[s][:, :], start=False, stop=True).then_inc(rank_made, 1)

                walk(pe, step, -1, B + 3, UN, head=8, tail=4)
                pe.wait_ge(msum_made, B)
                pe.matmul(bank[0][:, 0:NE], ones[:, :], msum[B % 2][:, :], start=True, stop=True).then_inc(counts_made, 1)

        XS = 8
        tile_in = sems(*[f"tile_in{s}" for s in range(XS)])
        y_out = sems(*[f"y_out{s}" for s in range(XS)])
        (tile_transposed, tile_t_copied, w1_ready, up_made, act_made, down_made, y_made) = sems(
            "tile_transposed", "tile_t_copied", "w1_ready", "up_made", "act_made", "down_made", "y_made")
        gathered = sems("gathered0", "gathered1")
        (row_steps,) = sems("row_steps")
        rows_in = sems("rows_in0", "rows_in1")
        final_out = sems("final_out0", "final_out1")
        (idx_ready, gates_copied, gates_transposed, gates_t_copied, bias_made, sum1, sum2, sum3, sum4, final_made) = sems(
            "idx_ready", "gates_copied", "gates_transposed", "gates_t_copied", "bias_made", "sum1", "sum2", "sum3",
            "sum4", "final_made")

        with ExitStack() as st2:
            def s2(name, shape, dt=F32):
                return sb(name, shape, dt, st2)

            NT = SHARED_TILES + ROUTED_TILES
            W = XS
            LEAD = 6
            xt = [s2(f"xt{i}", [P, D1]) for i in range(XS)]
            y_sb = [s2(f"y_sb{i}", [P, D1]) for i in range(XS)]
            xtt = [s2(f"xtt{i}", [P, 2 * P]) for i in range(2)]
            up = [s2(f"up{i}", [P, 2 * P]) for i in range(2)]
            w1b = [s2(f"w1b{i}", [P, 2 * INTER]) for i in range(2)]
            pick_w = s2("pick_w", [LQ, B * TOP, NE])
            row_w, slots_y = s2("row_w", [LQ, B * TOP]), s2("slots_y", [LQ, B, TOP], I32)
            sidx = [s2(f"sidx{i}", [LQ, TOP], I32) for i in range(2)]
            gb = [s2(f"gb{i}", [LQ, NE + 1]) for i in range(2)]
            gt = [s2(f"gt{i}", [NE + 1, LQ]) for i in range(2)]
            yk = [s2(f"yk{i}", [LQ, TOP, D1]) for i in range(2)]
            basr = [s2(f"basr{i}", [LQ, D1]) for i in range(2)]
            shr = [s2(f"shr{i}", [LQ, D1]) for i in range(2)]
            acc = [[s2(f"acc{k}_{i}", [LQ, D1]) for i in range(2)] for k in range(5)]

            tile_ps = [bank[0][:, 0:2 * P], bank[1][:, 0:2 * P]]
            up_ps = [bank[2][:, 0:2 * P], bank[3][:, 0:2 * P]]
            down_ps = [bank[4][:, 0:D1], bank[5][:, 0:D1]]
            gt_ps = [bank[0][0:NE + 1, 0:LQ], bank[1][0:NE + 1, 0:LQ]]
            bias_ps = [bank[2][0:LQ, 0:D1], bank[3][0:LQ, 0:D1]]

            def table_entry(eng, t, col, top):
                return eng.value_load(table[0:1, bass.ds(t.count(-SHARED_TILES), 1), col:col + 1].rearrange("a b c -> a (b c)"),
                                      min_val=0 if col == 0 else TOKENS, max_val=top)

            def out_rows(t):
                return ys[bass.ds(t.count() * P, P), :]

            block = st2.enter_context(nc.Block())

            @block.sync
            def _(sp):
                def load(t, routed):
                    s = t.slot(XS)
                    if t.has(XS):
                        sp.wait_ge(tile_transposed, t.count(1 - XS))
                    first = table_entry(sp, t, 1, LIST_END - P) if routed else t.count() * P
                    sp.dma_start(xt[s][:, :], xs[bass.ds(first, P), :]).then_inc(tile_in[s], 16)

                def store(t):
                    s = t.slot(XS)
                    sp.wait_ge(y_made, t.count(1))
                    sp.dma_start(out_rows(t), y_sb[s][:, :]).then_inc(y_out[s], 16)

                def both(routed):
                    def step(t):
                        load(t.back(-LEAD), routed)
                        store(t)
                    return step

                for s in range(SLOTS):
                    sp.wait_ge(h_out[s], B // SLOTS * 16)
                for t in range(LEAD):
                    load(At(0, t, W), False)
                walk(sp, both(False), 0, SHARED_TILES - LEAD, W, head=2)
                for s in range(SLOTS):
                    sp.wait_ge(scattered[s], B // SLOTS * TOP * 16)
                sp.wait_ge(pads_out, NE * 16)
                sp.wait_ge(table_in, 16)
                for t in range(SHARED_TILES - LEAD, SHARED_TILES):
                    both(True)(At(0, t, W))
                walk(sp, both(True), SHARED_TILES, NT - LEAD, W)
                for t in range(NT - LEAD, NT):
                    store(At(0, t, W))

                for s in range(SLOTS):
                    sp.wait_ge(base_out[s], B // SLOTS * 16)
                for s in range(XS):
                    sp.wait_ge(y_out[s], len(range(s, NT, XS)) * 16)

                def put(b):
                    s = b.slot(2)
                    sp.wait_ge(final_made, b.count(1))
                    sp.dma_start(out[bass.ds(b.count(), 1)].rearrange("o p n -> (o p) n"), acc[4][s][:, :])\
                      .then_inc(final_out[s], 16)

                def fetch(b):
                    s = b.slot(2)
                    if b.has(2):
                        sp.wait_ge(sum4, b.count(-1))
                    v = bass.ds(b.count(), 1)
                    sp.dma_start(basr[s][:, :], base_d[v].rearrange("o p n -> (o p) n")).then_inc(rows_in[s], 16)
                    sp.dma_start(shr[s][:, :], ys[0:TOKENS, :].rearrange("(b t) d -> b t d", t=LQ)[v]
                                 .rearrange("o p n -> (o p) n")).then_inc(rows_in[s], 16)
                    if b.has(1):
                        put(b.back(1))

                walk(sp, fetch, 0, B, 2, head=2)
                put(At(0, B - 1, 2))
                for s in range(2):
                    sp.wait_ge(final_out[s], B // 2 * 16)

            @block.gpsimd
            def _(pool):
                pool.wait_ge(row_steps, 4)
                for s in range(XS):
                    pool.wait_ge(y_out[s], len(range(s, NT, XS)) * 16)

                def gather(b):
                    s = b.slot(2)
                    if b.has(2):
                        pool.wait_ge(sum3, b.count(-1))
                    pool.tensor_copy(sidx[s][:, :], slots_y[:, bass.ds(b.count(), 1), :].rearrange("p o n -> p (o n)"))\
                        .then_inc(idx_ready, 1)
                    pool.wait_ge(idx_ready, b.count(1))
                    alone(pool)
                    for k in range(TOP):
                        pool.indirect_dma_start(yk[s][:, k, :], None, ys[:, :],
                                                bass.IndirectOffsetOnAxis(ap=sidx[s][:, k:k + 1], axis=0)).then_inc(gathered[s], 16)

                walk(pool, gather, 0, B, 2, head=2)

            @block.scalar
            def _(act):
                act.wait_ge(small_in, 64)

                def copy_t(t):
                    s = t.slot(2)
                    act.wait_ge(tile_transposed, t.count(1))
                    if t.has(2):
                        act.wait_ge(up_made, t.count(-1))
                    act.activation(xtt[s][:, :], tile_ps[s], ACT.Copy).then_inc(tile_t_copied, 1)

                def gelu(t, routed):
                    s = t.slot(2)
                    e = bass.ds(table_entry(act, t, 0, NE - 1) if routed else NE, 1)
                    act.wait_ge(up_made, t.count(1))
                    if t.has(2):
                        act.wait_ge(down_made, t.count(-1))
                    for m in range(2):
                        ins = act.activation(up[s][:, m * P:m * P + P], up_ps[s][:, m * P:m * P + P], ACT.Gelu,
                                             bias=b1_all[:, e, m:m + 1].rearrange("p o n -> p (o n)"))
                    ins.then_inc(act_made, 1)

                def both(routed):
                    def step(t):
                        copy_t(t.back(-1))
                        gelu(t, routed)
                    return step

                copy_t(At(0, 0, W))
                walk(act, both(False), 0, SHARED_TILES, W, head=2)
                act.wait_ge(table_in, 16)
                walk(act, both(True), SHARED_TILES, NT - 1, W)
                gelu(At(0, NT - 1, W), True)

                def gates(b):
                    s = b.slot(2)
                    act.wait_ge(gates_transposed, b.count(1))
                    if b.has(2):
                        act.wait_ge(bias_made, b.count(-1))
                    act.activation(gt[s][:, :], gt_ps[s], ACT.Copy).then_inc(gates_t_copied, 1)

                walk(act, gates, 0, B, 2, head=2)

            @block.vector
            def _(dve):
                def evac(t):
                    s = t.slot(2)
                    dve.wait_ge(down_made, t.count(1))
                    if t.has(XS):
                        dve.wait_ge(y_out[t.slot(XS)], t.turn(XS) * 16)
                    dve.tensor_copy(y_sb[t.slot(XS)][:, :], down_ps[s]).then_inc(y_made, 1)

                def step(t):
                    n = t.back(-2)
                    e = table_entry(dve, n, 0, NE - 1)
                    if n.has(SHARED_TILES + 2):
                        dve.wait_ge(up_made, n.count(-1))
                    dve.tensor_copy(w1b[n.slot(2)][:, :], w1_all[:, bass.ds(e, 1), :].rearrange("p o n -> p (o n)"))\
                       .then_inc(w1_ready, 1)
                    evac(t)

                four = [LQ, B, TOP, NE]
                pick4 = pick_w[:, :, :].rearrange("p (b k) e -> p b k e", k=TOP)
                dve.tensor_tensor(pick4, rec_all[:, :, NE + 8:REC].unsqueeze(3).to_broadcast(four),
                                  iota_e[:, :].unsqueeze(1).unsqueeze(1).to_broadcast(four), ALU.is_equal).then_inc(row_steps, 1)
                for t in range(2):
                    evac(At(0, t, W))
                dve.wait_ge(row_steps, 1)
                dve.tensor_tensor(pick_w[:, :, :], pick_w[:, :, :], shift[0:LQ, :].unsqueeze(1).to_broadcast([LQ, B * TOP, NE]),
                                  ALU.mult).then_inc(row_steps, 1)
                for t in range(2, 4):
                    evac(At(0, t, W))
                dve.wait_ge(row_steps, 2)
                dve.tensor_reduce(row_w[:, :], pick_w[:, :, :], AX.X, ALU.add).then_inc(row_steps, 1)
                for t in range(4, 6):
                    evac(At(0, t, W))
                dve.wait_ge(row_steps, 3)
                dve.tensor_tensor(slots_y[:, :, :].rearrange("p b k -> p (b k)"), row_w[:, :],
                                  slots_all[:, :, :].rearrange("p b k -> p (b k)"), ALU.add).then_inc(row_steps, 1)
                walk(dve, evac, 6, SHARED_TILES - 2, W, head=2)
                dve.wait_ge(expert_in, 16 * 2 * B)
                dve.wait_ge(table_in, 16)
                walk(dve, step, SHARED_TILES - 2, NT - 2, W, head=2)
                for t in range(NT - 2, NT):
                    evac(At(0, t, W))

                def combine(b):
                    s = b.slot(2)
                    if b.has(2):
                        dve.wait_ge(gates_transposed, b.count(-1))
                    dve.tensor_copy(gb[s][:, :], gates_all[:, bass.ds(b.count(), 1), :].rearrange("p o n -> p (o n)"))\
                       .then_inc(gates_copied, 1)
                    dve.wait_ge(rows_in[s], b.turn(2, 1) * 32)
                    dve.wait_ge(gathered[s], b.turn(2, 1) * (16 * TOP))
                    last = basr[s]
                    for k, done in enumerate((sum1, sum2, sum3)):
                        dve.scalar_tensor_tensor(acc[k][s][:, :], yk[s][:, k, :],
                                                 gate_k[:, bass.ds(b.count(), 1), k:k + 1].rearrange("p o n -> p (o n)"),
                                                 last[:, :], ALU.mult, ALU.add).then_inc(done, 1)
                        dve.wait_ge(done, b.count(1))
                        last = acc[k][s]
                    dve.tensor_tensor(acc[3][s][:, :], last[:, :], shr[s][:, :], ALU.add).then_inc(sum4, 1)
                    dve.wait_ge(sum4, b.count(1))
                    dve.wait_ge(bias_made, b.count(1))
                    if b.has(2):
                        dve.wait_ge(final_out[s], b.turn(2) * 16)
                    dve.tensor_tensor(acc[4][s][:, :], acc[3][s][:, :], bias_ps[s], ALU.add).then_inc(final_made, 1)

                walk(dve, combine, 0, B, 2, head=2)

            @block.tensor
            def _(pe):
                pe.wait_ge(expert_in, 16 * 2 * B)

                def transposes(t):
                    s, sx = t.slot(2), t.slot(XS)
                    pe.wait_ge(tile_in[sx], t.turn(XS, 1) * 16)
                    if t.has(2):
                        pe.wait_ge(tile_t_copied, t.count(-1))
                    for c in range(2):
                        mm = pe.transpose(tile_ps[s][:, c * P:c * P + P], xt[sx][:, c * P:c * P + P], ident[:, :])
                    mm.then_inc(tile_transposed, 1)

                def up_product(t, routed):
                    s = t.slot(2)
                    pe.wait_ge(tile_t_copied, t.count(1))
                    if t.has(2):
                        pe.wait_ge(act_made, t.count(-1))
                    if routed:
                        pe.wait_ge(w1_ready, t.count(1 - SHARED_TILES))
                    w = w1b[s] if routed else w1_all[:, NE, :]
                    for m in range(2):
                        for c in range(2):
                            mm = pe.matmul(up_ps[s][:, m * P:m * P + P], w[:, c * INTER + m * P:c * INTER + m * P + P],
                                           xtt[s][:, c * P:c * P + P], start=(c == 0), stop=(c == 1))
                    mm.then_inc(up_made, 1)

                def down_product(t, routed):
                    s = t.slot(2)
                    e = bass.ds(table_entry(pe, t, 0, NE - 1) if routed else NE, 1)
                    pe.wait_ge(act_made, t.count(1))
                    if t.has(2):
                        pe.wait_ge(y_made, t.count(-1))
                    for m in range(2):
                        w = w2_all[:, e, m * D1:(m + 1) * D1].rearrange("p o n -> p (o n)")
                        mm = pe.matmul(down_ps[s], up[s][:, m * P:m * P + P], w, start=(m == 0), stop=(m == 1))
                    mm.then_inc(down_made, 1)

                def three(up_routed, down_routed):
                    def step(t):
                        transposes(t.back(-2))
                        up_product(t.back(-1), up_routed)
                        down_product(t, down_routed)
                    return step

                transposes(At(0, 0, W))
                transposes(At(0, 1, W))
                up_product(At(0, 0, W), False)
                walk(pe, three(False, False), 0, SHARED_TILES - 1, W, head=2)
                pe.wait_ge(table_in, 16)
                three(True, False)(At(0, SHARED_TILES - 1, W))
                walk(pe, three(True, True), SHARED_TILES, NT - 2, W)
                up_product(At(0, NT - 1, W), True)
                down_product(At(0, NT - 2, W), True)
                down_product(At(0, NT - 1, W), True)

                def bias_rows(b):
                    s = b.slot(2)
                    pe.wait_ge(gates_copied, b.count(1))
                    if b.has(2):
                        pe.wait_ge(gates_t_copied, b.count(-1))
                    pe.transpose(gt_ps[s], gb[s][:, :], ident[0:LQ, 0:LQ]).then_inc(gates_transposed, 1)
                    pe.wait_ge(gates_t_copied, b.count(1))
                    if b.has(2):
                        pe.wait_ge(final_made, b.count(-1))
                    pe.matmul(bias_ps[s], gt[s][:, :], b2_all[:, :], start=True, stop=True).then_inc(bias_made, 1)

                walk(pe, bias_rows, 0, B, 2, head=2)


def kernel(**inputs):
    import numpy as np
    import concourse.bacc as bacc
    from concourse.bass_utils import run_bass_kernel_spmd

    get = {k.replace("L0_xattn_", "").replace("L0_ffn_", "ffn_"): np.asarray(v) for k, v in inputs.items()}

    def column(v, n=2):
        return v.reshape(n, -1).T

    def expert(shared, each):
        w = np.concatenate([each, shared[None]])
        return w.reshape(w.shape[0], 2, P, w.shape[2]).transpose(0, 2, 1, 3).reshape(w.shape[0], P, -1)

    be1 = np.concatenate([get["ffn_Be1"], get["ffn_bs1"][None]])
    arrays = {
        "x": get["x"], "ctx": get["ctx_768"],
        "g1c": column(get["ln1_g"]), "b1c": column(get["ln1_b"]),
        "g2c": get["ln2_g"][:, None], "b2c": get["ln2_b"][:, None],
        "wq": get["Wq"], "wqt": get["Wq"].T, "bqc": column(get["bq"]),
        "wk": get["Wk"], "wkt": get["Wk"].T, "bkc": column(get["bk"]),
        "wv": get["Wv"], "wvt": get["Wv"].T, "bvc": column(get["bv"]),
        "wo": get["Wo"], "bo": get["bo"][None],
        "w1": expert(get["ffn_ws1"], get["ffn_We1"]),
        "be1": be1.reshape(NE + 1, 2, P).transpose(2, 0, 1),
        "w2": expert(get["ffn_ws2"], get["ffn_We2"]),
        "b2": np.concatenate([get["ffn_Be2"], get["ffn_bs2"][None]]),
        "wr": get["ffn_Wr"], "br": get["ffn_br"],
    }
    nc = bacc.Bacc("TRN2", target_bir_lowering=False, num_devices=1)
    args, given = [], {}
    for name, a in arrays.items():
        a = np.ascontiguousarray(a)
        given[f"in_{name}"] = a
        args.append(nc.dram_tensor(f"in_{name}", a.shape, mybir.dt.from_np(a.dtype), kind="ExternalInput").ap())
    args.append(nc.dram_tensor("out_0", (B, LQ, D1), F32, kind="ExternalOutput").ap())
    program(nc, *args)
    r = run_bass_kernel_spmd(nc, [given], core_ids=[0])
    return r.results[0]["out_0"]
```

```python
import concourse.bass as bass
from concourse import mybir
from contextlib import ExitStack

F32 = mybir.dt.float32
BF16 = mybir.dt.bfloat16
I32 = mybir.dt.int32
U32 = mybir.dt.uint32
ALU = mybir.AluOpType
ACT = mybir.ActivationFunctionType
AX = mybir.AxisListType

P = 128
B, LQ, LK = 32, 100, 361
D1, D2, E = 256, 192, 256
NE, TOP = 31, 3
INTER = 256
EPS = 1e-5
SCALE = float(E) ** -0.5

D2B = D2 - P
D2C = D2B + 1
KT = [P, P, LK - 2 * P]
TOKENS = B * LQ
SHARED_TILES = TOKENS // P
CAP = TOKENS + P
ROUTED_TILES = (TOKENS * TOP - NE) // P + NE
LIST_END = TOKENS + NE * CAP
REC = NE + 8
WHO, EXPS, SUM, TOKEN = D1, D1 + TOP, D1 + 2 * TOP, D1 + 2 * TOP + 1
ROW = TOKEN + 1

UN = 4
SLOTS = 4


class At:

    def __init__(self, j, r, n):
        self.j, self.r, self.n = j, r, n
        self.fixed = isinstance(j, int)

    def back(self, k):
        return At(self.j, self.r - k, self.n)

    def count(self, k=0):
        assert self.r + k >= 0
        return self.r + k if self.fixed else self.j * self.n + (self.r + k)

    def has(self, k):
        assert self.fixed or self.r >= k
        return self.r >= k

    def slot(self, m):
        return self.r % m

    def turn(self, m, k=0):
        assert self.r // m + k >= 0
        return self.r // m + k if self.fixed else self.j * (self.n // m) + (self.r // m + k)


def alone(eng):
    eng.nop(nofuse=True)


def walk(eng, step, lo, hi, n, head=0, tail=0):
    for i in range(lo, lo + head):
        step(At(0, i, n))
    passes = (hi - lo - head - tail) // n
    assert passes > 0, (lo, hi, n, head, tail)
    with eng.Fori(0, passes) as j:
        for r in range(lo + head, lo + head + n):
            step(At(j, r, n))
    for i in range(lo + head + n * passes, hi):
        step(At(0, i, n))


def program(nc, x, ctx_t, g1c, b1c, g2c, b2c, wq, wqt, bqc, wk, wkt, bkc, wv, wvt, bvc, wo, bo,
            w1, be1, w2, b2, wr, br, out):
    xs = nc.dram_tensor("expert_rows_in", [LIST_END + P, ROW], F32, kind="Internal").ap()
    sums = [nc.dram_tensor(f"sum{k}", [TOKENS + P, D1], F32, kind="Internal").ap() for k in range(2)]
    tab_d = nc.dram_tensor("tile_table", [2, ROUTED_TILES], I32, kind="Internal").ap()
    x4 = x.rearrange("(q s) t d -> s q t d", s=SLOTS)
    c4 = ctx_t.rearrange("(q s) t d -> s q t d", s=SLOTS)
    h4 = xs[0:TOKENS, 0:D1].rearrange("(q s t) d -> s q t d", s=SLOTS, t=LQ)
    base4 = sums[0][0:TOKENS, :].rearrange("(q s t) d -> s q t d", s=SLOTS, t=LQ)
    w1_4 = w1.rearrange("(q s) p n -> s q p n", s=SLOTS)
    w2_4 = w2.rearrange("(q s) p n -> s q p n", s=SLOTS)

    stack = ExitStack()
    with stack:
        def sb(name, shape, dt=F32, st=stack):
            return st.enter_context(nc.sbuf_tensor(name, shape, dt))

        def sems(*names):
            return [stack.enter_context(nc.semaphore(n)) for n in names]

        w1_all = sb("w1_all", [P, NE + 1, 2 * INTER])
        w2_all = sb("w2_all", [P, NE + 1, 2 * D1])
        b1_all = sb("b1_all", [P, NE + 1, 2])
        b2_all = sb("b2_all", [NE + 1, D1])
        ident = sb("ident", [P, P])
        idx_all = sb("idx_all", [LQ, B, TOP])
        gates_all = sb("gates_all", [LQ, B, NE + 1])
        msum = [sb(f"msum{i}", [LQ, NE], BF16) for i in range(2)]
        ones = sb("ones", [LQ, P], BF16)
        iota_slot, tile_no = sb("iota_slot", [P, NE]), sb("tile_no", [P, 1])
        table = sb("table", [1, 2, ROUTED_TILES], I32)
        iota_e = sb("iota_e", [LQ, NE])
        pad_row = sb("pad_row", [1, NE], I32)
        pad_rows = sb("pad_rows", [P, ROW])
        bank = [stack.enter_context(nc.psum_tensor(f"bank{i}", [P, 512], F32)) for i in range(8)]
        idx4 = idx_all[:, :, :].rearrange("p (q s) n -> p s q n", s=SLOTS)
        gates4 = gates_all[:, :, :].rearrange("p (q s) n -> p s q n", s=SLOTS)
        w1_all4 = w1_all[:, :, :].rearrange("p (q s) n -> p s q n", s=SLOTS)
        w2_all4 = w2_all[:, :, :].rearrange("p (q s) n -> p s q n", s=SLOTS)

        weights_in, expert_in, made, small_in = sems("weights_in", "expert_in", "made", "small_in")
        x_in = sems(*[f"x_in{s}" for s in range(SLOTS)])
        xr_in = sems(*[f"xr_in{s}" for s in range(SLOTS)])
        c_in = sems(*[f"c_in{s}" for s in range(SLOTS)])
        h_out = sems(*[f"h_out{s}" for s in range(SLOTS)])
        base_out = sems(*[f"base_out{s}" for s in range(SLOTS)])
        scattered = sems(*[f"scattered{s}" for s in range(SLOTS)])
        (cols_ready, aug_ready, folds_made, folds_ready, ctx_stat6, ctx_stats, ctx_var, ctx_rstd, ctx_norm,
         x_stat6, x_norm) = sems(
            "cols_ready", "aug_ready", "folds_made", "folds_ready", "ctx_stat6", "ctx_stats", "ctx_var", "ctx_rstd",
            "ctx_norm", "x_stat6", "x_norm")
        (ctx_transposed, ctx_t_copied, x_transposed, x_t_copied, q_made, q_copied, scores_made, rowmax_made,
         probs_made, rinv_made, probs_transposed, probs_t_copied, mix_made, mix_copied, attn_made,
         resid_made, resid_stat6, resid_stats, resid_var, resid_rstd, h_made) = sems(
            "ctx_transposed", "ctx_t_copied", "x_transposed", "x_t_copied", "q_made", "q_copied", "scores_made",
            "rowmax_made", "probs_made", "rinv_made", "probs_transposed", "probs_t_copied", "mix_made",
            "mix_copied", "attn_made", "resid_made", "resid_stat6", "resid_stats", "resid_var", "resid_rstd",
            "h_made")
        (h_transposed, h_t_copied, logits_made, logit_sum, top_vals, top_idx, idx_float, picks_made, mask_made,
         msum_made, neg_made, meta_made, rank_made, slot_sum, slot_picks, slots_made) = sems(
            "h_transposed", "h_t_copied", "logits_made", "logit_sum", "top_vals", "top_idx", "idx_float",
            "picks_made", "mask_made", "msum_made", "neg_made", "meta_made", "rank_made", "slot_sum", "slot_picks",
            "slots_made")
        counts_made, dve_chain, late_steps, pads_ready, pads_out, table_made, table_out, table_in = sems(
            "counts_made", "dve_chain", "late_steps", "pads_ready", "pads_out", "table_made", "table_out", "table_in")

        with ExitStack() as st1:
            def s1(name, shape, dt=F32):
                return sb(name, shape, dt, st1)

            wq_s, wqt_s, wo_s, wk_s, wv_s, bo_s, wk_aug, wv_aug = (
                w2_all[:, NE - 7 + k, :].rearrange("p (c n) -> p c n", c=2) for k in range(8))
            wk0, wk1, wv0, wv1 = wk_s[:, 0, :], wk_s[0:D2B, 1, :], wv_s[:, 0, :], wv_s[0:D2B, 1, :]
            bo_row = bo_s[0:D2C, 0, :]
            wk_aug, wv_aug = wk_aug[:, :, 0:D2 + 1], wv_aug[:, :, 0:D2 + 1]
            g1_s, b1_s, bq_s, bk_s, bv_s = (s1(n, [P, 2]) for n in ("g1_s", "b1_s", "bq_s", "bk_s", "bv_s"))
            g2_0, g2_1, b2_0, b2_1 = (s1("g2_0", [P, 1]), s1("g2_1", [D2C, 1]), s1("b2_0", [P, 1]),
                                      s1("b2_1", [D2B, 1]))
            uq = s1("uq", [P, 2])
            fold_q = s1("fold_q", [P, 2, D2 + 1])
            fold_o0, fold_o1 = s1("fold_o0", [P, D1]), s1("fold_o1", [D2C, D1])
            qs0, qs1 = s1("qs0", [P, 2]), s1("qs1", [D2C, 2])
            wr_s = s1("wr_s", [P, 2, NE])
            br_s = s1("br_s", [LQ, NE])
            tri = s1("tri", [LQ, LQ], BF16)
            mhalf, eps_cols = s1("mhalf", [P, 4]), s1("eps_cols", [P, 4])
            c_sb = [s1(f"c_sb{i}", [P, 3, D2]) for i in range(SLOTS)]
            z = [s1(f"z{i}", [P, 3, D2 + 1]) for i in range(SLOTS)]
            x_sb = [s1(f"x_sb{i}", [LQ, D1]) for i in range(SLOTS)]
            xr_sb = [s1(f"xr_sb{i}", [LQ, D1]) for i in range(SLOTS)]
            h_sb = [s1(f"h_sb{i}", [LQ, ROW]) for i in range(SLOTS)]
            negtop = [s1(f"negtop{i}", [LQ, 1]) for i in range(2)]
            token_no = s1("token_no", [LQ, B])
            token4 = token_no[:, :].rearrange("p (q s) -> p s q", s=SLOTS)

            def two(name, shape, dt=F32):
                return [s1(f"{name}{i}", shape, dt) for i in range(2)]

            c6, x6, mv, rs = two("c6", [P, 3, 6]), two("x6", [LQ, 6]), two("mv", [P, 4, 2]), two("rs", [P, 2, 4])
            r6, rmv, rrs = two("r6", [LQ, 6]), two("rmv", [LQ, 2]), two("rrs", [LQ, 2])
            z1, z1t = two("z1", [LQ, D1]), two("z1t", [P, 2 * LQ])
            qt0, qt1 = two("qt0", [P, LQ]), two("qt1", [D2C, LQ])
            zt0, zt1 = two("zt0", [P, LK]), two("zt1", [D2C, LK])
            probs, probs_t = two("probs", [LQ, LK]), two("probs_t", [P, 3, LQ])
            negmax, rowsum, rinv = two("negmax", [LQ, 1]), two("rowsum", [LQ, 1]), two("rinv", [LQ, 1])
            mix0, mix1 = two("mix0", [P, LQ]), two("mix1", [D2C, LQ])
            resid = [s1(f"resid{i}", [LQ, D1]) for i in range(SLOTS)]
            h_t = two("h_t", [P, 2 * LQ])
            rec, idx8 = two("rec", [LQ, REC]), two("idx8", [LQ, 8], U32)
            picks, mask = two("picks", [LQ, TOP, NE]), two("mask", [LQ, NE], BF16)
            slotf, slotp, slot = two("slotf", [LQ, NE]), two("slotp", [LQ, TOP, NE]), two("slot", [LQ, TOP], I32)
            MADE = 26

            zt_ps0, zt_ps1 = bank[2], bank[3]
            probs_ps, rank_ps = bank[4][:, 0:3 * LQ], bank[4][0:LQ, 320:320 + NE]
            mix_ps, attn_ps = bank[5][:, 0:2 * LQ], bank[5][0:LQ, 256:512]
            z1_ps, q_ps = bank[6][:, 0:2 * LQ], bank[6][:, 256:256 + 2 * LQ]
            h_ps, logit_ps = bank[7][:, 0:2 * LQ], bank[7][0:LQ, 256:256 + NE]

            def inside(b):
                return not b.fixed or 0 <= b.r < B

            def rows(v4, b):
                return v4[b.slot(SLOTS), bass.ds(b.turn(SLOTS), 1)].rearrange("o p n -> (o p) n")

            block = st1.enter_context(nc.Block())

            @block.sync
            def _(sp):
                for dst, src in (
                    (wq_s[:, :, :], wq.rearrange("(c p) e -> p c e", p=P)), (wqt_s[:, :, :], wqt.rearrange("(c p) e -> p c e", p=P)),
                    (wk0[:, :], wk[0:P, :]), (wk1[:, :], wk[P:D2, :]), (wv0[:, :], wv[0:P, :]), (wv1[:, :], wv[P:D2, :]),
                    (wk_aug[:, :, 0:D2], wkt.rearrange("(c p) e -> p c e", p=P)),
                    (wv_aug[:, :, 0:D2], wvt.rearrange("(c p) e -> p c e", p=P)),
                    (wo_s[:, :, :], wo.rearrange("(c p) e -> p c e", p=P)), (bo_row[D2B:D2C, :], bo),
                    (g1_s[:, :], g1c), (b1_s[:, :], b1c), (bq_s[:, :], bqc), (bk_s[:, :], bkc), (bv_s[:, :], bvc),
                    (g2_0[:, :], g2c[0:P, :]), (g2_1[0:D2B, :], g2c[P:D2, :]),
                    (b2_0[:, :], b2c[0:P, :]), (b2_1[:, :], b2c[P:D2, :]),
                ):
                    sp.dma_start(dst, src).then_inc(weights_in, 16)

                def load_x(b):
                    if b.has(SLOTS):
                        sp.wait_ge(x_norm, b.count(1 - SLOTS))
                        alone(sp)
                    sp.dma_start(x_sb[b.slot(SLOTS)][:, :], rows(x4, b)).then_inc(x_in[b.slot(SLOTS)], 16)

                def load_ctx(b):
                    if b.has(SLOTS):
                        sp.wait_ge(ctx_norm, b.count(1 - SLOTS))
                        alone(sp)
                    src = rows(c4, b)
                    s = b.slot(SLOTS)
                    sp.dma_start(c_sb[s][:, 0:2, :], src[0:2 * P, :].rearrange("(t p) d -> p t d", p=P)).then_inc(c_in[s], 16)
                    sp.dma_start(c_sb[s][0:KT[2], 2, :], src[2 * P:LK, :]).then_inc(c_in[s], 16)

                def load_resid(b):
                    if b.has(SLOTS):
                        sp.wait_ge(resid_made, b.count(1 - SLOTS))
                        alone(sp)
                    sp.dma_start(xr_sb[b.slot(SLOTS)][:, :], rows(x4, b)).then_inc(xr_in[b.slot(SLOTS)], 16)

                sp.wait_ge(made, MADE)
                for b in range(2):
                    load_ctx(At(0, b, UN))
                    load_x(At(0, b, UN))

                def step(i):
                    b = i.back(-4)
                    if inside(b):
                        load_ctx(b)
                        load_x(b)
                    b = i.back(-1)
                    if inside(b):
                        load_resid(b)
                        s = b.slot(SLOTS)
                        sp.dma_start(w1_all4[:, s, bass.ds(b.turn(SLOTS), 1), :].rearrange("p o n -> p (o n)"),
                                     rows(w1_4, b)).then_inc(expert_in, 16)
                        sp.dma_start(w2_all4[:, s, bass.ds(b.turn(SLOTS), 1), :].rearrange("p o n -> p (o n)"),
                                     rows(w2_4, b)).then_inc(expert_in, 16)
                    b = i.back(4)
                    if inside(b):
                        sp.wait_ge(h_made, b.count(1))
                        alone(sp)
                        sp.dma_start(rows(h4, b), h_sb[b.slot(SLOTS)][:, 0:D1]).then_inc(h_out[b.slot(SLOTS)], 16)
                        sp.dma_start(rows(base4, b), resid[b.slot(SLOTS)][:, :]).then_inc(base_out[b.slot(SLOTS)], 16)

                walk(sp, step, -2, B + 4, UN, head=10, tail=8)

            @block.gpsimd
            def _(pool):
                n = [0]

                def const(ins):
                    n[0] += 1
                    ins.then_inc(made, 1)
                    return n[0]

                const(pool.memset(mhalf[:, :], -0.5))
                const(pool.memset(eps_cols[:, 0:3], EPS))
                const(pool.memset(eps_cols[:, 3:4], EPS * EPS / (1.0 + EPS)))
                for s in range(2):
                    const(pool.memset(mv[s][:, :, :], 1.0))
                for s in range(SLOTS):
                    const(pool.memset(c_sb[s][:, :, :], 0.0))
                for s in range(SLOTS):
                    const(pool.memset(z[s][:, :, D2:D2 + 1], 1.0))
                const(pool.memset(msum[0][:, :], 0.0))
                const(pool.memset(ones[:, :], 1.0))
                const(pool.iota(iota_e[:, :], pattern=[[1, NE]], base=0, channel_multiplier=0,
                                allow_small_or_imprecise_dtypes=True))
                const(pool.iota(iota_slot[:, :], pattern=[[CAP, NE]], base=TOKENS, channel_multiplier=0,
                                allow_small_or_imprecise_dtypes=True))
                const(pool.iota(tile_no[:, :], pattern=[[0, 1]], base=0, channel_multiplier=1,
                                allow_small_or_imprecise_dtypes=True))
                const(pool.memset(pad_rows[:, 0:SUM], 0.0))
                const(pool.memset(pad_rows[:, SUM:SUM + 1], 1.0))
                const(pool.iota(pad_rows[:, TOKEN:TOKEN + 1], pattern=[[0, 1]], base=TOKENS, channel_multiplier=1,
                                allow_small_or_imprecise_dtypes=True))
                const(pool.iota(token_no[:, :], pattern=[[LQ, B]], base=0, channel_multiplier=1,
                                allow_small_or_imprecise_dtypes=True))
                const(pool.memset(ident[:, :], 0.0))
                k = const(pool.memset(tri[:, :], 1.0))
                pool.wait_ge(made, k)
                const(pool.affine_select(out=ident[:, :], in_=ident[:, :], compare_op=ALU.not_equal, fill=1.0,
                                         base=0, pattern=[[-1, P]], channel_multiplier=1))
                k = const(pool.affine_select(out=tri[:, :], in_=tri[:, :], compare_op=ALU.is_gt, fill=0.0,
                                             base=0, pattern=[[1, LQ]], channel_multiplier=-1))
                assert k == MADE, k
                pool.dma_start(wr_s[:, :, :], wr.rearrange("(c p) e -> p c e", p=P)).then_inc(small_in, 16)
                pool.dma_start(br_s[:, :], br.partition_broadcast(LQ)).then_inc(small_in, 16)
                pool.dma_start(b1_all[:, :, :], be1).then_inc(small_in, 16)
                pool.dma_start(b2_all[:, :], b2).then_inc(small_in, 16)

                pool.wait_ge(made, MADE)

                def step(i):
                    b = i.back(-2)
                    if inside(b):
                        s = b.slot(2)
                        pool.wait_ge(ctx_stats, b.count(1))
                        pool.tensor_tensor(rs[s][:, 0, :], mv[s][:, :, 1], eps_cols[:, :], ALU.add).then_inc(ctx_var, 1)
                        pool.wait_ge(ctx_var, b.count(1))
                        pool.tensor_tensor(rs[s][:, 1, :], rs[s][:, 0, :], mhalf[:, :], ALU.pow).then_inc(ctx_rstd, 1)
                    b = i.back(4)
                    if inside(b):
                        s = b.slot(2)
                        pool.wait_ge(mask_made, b.count(1))
                        if b.has(1):
                            pool.wait_ge(rank_made, b.count(0))
                            pool.wait_ge(msum_made, b.count(0))
                        pool.tensor_tensor(msum[1 - s][:, :], msum[s][:, :], mask[s][:, :], ALU.add).then_inc(msum_made, 1)
                    b = i.back(2)
                    if inside(b):
                        s = b.slot(2)
                        pool.wait_ge(resid_stats, b.count(1))
                        pool.tensor_tensor(rrs[s][:, 0:1], rmv[s][:, 1:2], eps_cols[0:LQ, 0:1], ALU.add).then_inc(resid_var, 1)
                        pool.wait_ge(resid_var, b.count(1))
                        pool.tensor_tensor(rrs[s][:, 1:2], rrs[s][:, 0:1], mhalf[0:LQ, 0:1], ALU.pow).then_inc(resid_rstd, 1)
                    b = i.back(4)
                    if inside(b):
                        s, s4 = b.slot(2), b.slot(SLOTS)
                        pool.wait_ge(slots_made, b.count(1))
                        pool.wait_ge(meta_made, b.count(1))
                        if b.has(SLOTS):
                            pool.wait_ge(scattered[s4], b.turn(SLOTS) * (16 * TOP))
                        alone(pool)
                        for k in range(TOP):
                            pool.indirect_dma_start(xs, bass.IndirectOffsetOnAxis(ap=slot[s][:, k:k + 1], axis=0),
                                                    h_sb[s4][:, :], None).then_inc(scattered[s4], 16)

                walk(pool, step, -2, B + 4, UN, head=10, tail=8)

            @block.scalar
            def _(act):
                act.wait_ge(folds_ready, 1)

                def step(i):
                    b = i.back(2)
                    if inside(b):
                        s = b.slot(2)
                        act.wait_ge(probs_transposed, b.count(1))
                        if b.has(2):
                            act.wait_ge(mix_made, b.count(-1))
                        act.activation(probs_t[s][:, 0:2, :], probs_ps[:, 0:2 * LQ].rearrange("p (t q) -> p t q", q=LQ), ACT.Copy)
                        act.activation(probs_t[s][0:KT[2], 2, :], probs_ps[0:KT[2], 2 * LQ:3 * LQ],
                                       ACT.Copy).then_inc(probs_t_copied, 1)
                    b = i
                    if inside(b):
                        s = b.slot(2)
                        act.wait_ge(x_transposed, b.count(1))
                        if b.has(2):
                            act.wait_ge(q_made, b.count(-1))
                        act.activation(z1t[s][:, :], z1_ps, ACT.Copy).then_inc(x_t_copied, 1)
                    b = i
                    if inside(b):
                        s = b.slot(2)
                        act.wait_ge(ctx_transposed, b.count(1))
                        if b.has(2):
                            act.wait_ge(scores_made, b.count(-1))
                        act.activation(zt0[s][:, :], zt_ps0[:, 0:LK], ACT.Copy)
                        act.activation(zt1[s][:, :], zt_ps1[0:D2C, 0:LK], ACT.Copy).then_inc(ctx_t_copied, 1)
                    b = i.back(2)
                    if inside(b):
                        s = b.slot(2)
                        act.wait_ge(mix_made, b.count(1))
                        if b.has(2):
                            act.wait_ge(attn_made, b.count(-1))
                        act.activation(mix0[s][:, :], mix_ps[:, 0:LQ], ACT.Copy)
                        act.activation(mix1[s][:, :], mix_ps[0:D2C, LQ:2 * LQ], ACT.Copy).then_inc(mix_copied, 1)
                    b = i.back(1)
                    if inside(b):
                        s = b.slot(2)
                        act.wait_ge(rowmax_made, b.count(1))
                        if b.has(2):
                            act.wait_ge(probs_transposed, b.count(-1))
                            act.wait_ge(rinv_made, b.count(-1))
                        act.activation(probs[s][:, :], bank[s][0:LQ, 0:LK], ACT.Exp, bias=negmax[s][:, 0:1],
                                       accum_out=rowsum[s][:, 0:1]).then_inc(probs_made, 1)
                    b = i.back(4)
                    if inside(b):
                        s = b.slot(2)
                        act.wait_ge(top_vals, b.count(1))
                        act.activation(negtop[s][:, :], rec[s][:, NE:NE + 1], ACT.Copy, scale=-1.0).then_inc(neg_made, 1)
                    b = i.back(3)
                    if inside(b):
                        s = b.slot(2)
                        act.wait_ge(h_transposed, b.count(1))
                        if b.has(2):
                            act.wait_ge(logits_made, b.count(-1))
                        act.activation(h_t[s][:, :], h_ps, ACT.Copy).then_inc(h_t_copied, 1)
                    b = i
                    if inside(b):
                        s = b.slot(2)
                        act.wait_ge(q_made, b.count(1))
                        if b.has(2):
                            act.wait_ge(scores_made, b.count(-1))
                        act.activation(qt0[s][:, :], q_ps[:, 0:LQ], ACT.Identity, bias=qs0[:, 1:2], scale=qs0[:, 0:1])
                        act.activation(qt1[s][:, :], q_ps[0:D2C, LQ:2 * LQ], ACT.Identity, bias=qs1[:, 1:2],
                                       scale=qs1[:, 0:1]).then_inc(q_copied, 1)
                    b = i.back(4)
                    if inside(b):
                        s, s4 = b.slot(2), b.slot(SLOTS)
                        turn = bass.ds(b.turn(SLOTS), 1)
                        act.wait_ge(neg_made, b.count(1))
                        alone(act)
                        act.activation(gates4[:, s4, turn, 0:NE].rearrange("p o n -> p (o n)"), rec[s][:, 0:NE], ACT.Exp,
                                       bias=negtop[s][:, 0:1], accum_out=h_sb[s4][:, SUM:SUM + 1])
                        act.activation(h_sb[s4][:, EXPS:EXPS + TOP], rec[s][:, NE:NE + TOP], ACT.Exp, bias=negtop[s][:, 0:1])
                        act.activation(h_sb[s4][:, TOKEN:TOKEN + 1], token4[:, s4, turn], ACT.Copy)
                        act.wait_ge(idx_float, b.count(1))
                        alone(act)
                        act.activation(h_sb[s4][:, WHO:WHO + TOP], idx4[:, s4, turn, :].rearrange("p o n -> p (o n)"),
                                       ACT.Copy).then_inc(meta_made, 1)

                walk(act, step, 0, B + 4, UN, head=8, tail=4)

            @block.vector
            def _(dve):
                def step(i):
                    new, met, rated, mixed, added, routed = (i.back(k) for k in (-2, -1, 1, 2, 3, 4))
                    n2, n4 = new.slot(2), new.slot(SLOTS)
                    m2, m4 = mixed.slot(2), mixed.slot(SLOTS)
                    r2 = routed.slot(2)
                    if inside(routed):
                        chosen = idx4[:, routed.slot(SLOTS), bass.ds(routed.turn(SLOTS), 1), :].rearrange("p o n -> p (o n)")
                    if inside(routed):
                        dve.wait_ge(logits_made, routed.count(1))
                        if routed.has(2):
                            dve.wait_ge(meta_made, routed.count(-1))
                        dve.tensor_tensor(rec[r2][:, 0:NE], logit_ps, br_s[:, :], ALU.add).then_inc(logit_sum, 1)
                    if inside(new):
                        dve.wait_ge(c_in[n4], new.turn(SLOTS, 1) * 32)
                        for t in range(3):
                            ins = dve.bn_stats(c6[n2][:, t, :], c_sb[n4][:, t, :])
                        ins.then_inc(ctx_stat6, 1)
                    if inside(routed):
                        dve.wait_ge(logit_sum, routed.count(1))
                        alone(dve)
                        dve.max(rec[r2][:, NE:NE + 8], rec[r2][:, 0:NE]).then_inc(top_vals, 1)
                    if inside(added):
                        a2, a4 = added.slot(2), added.slot(SLOTS)
                        dve.wait_ge(resid_rstd, added.count(1))
                        if added.has(SLOTS):
                            o = added.back(SLOTS)
                            dve.wait_ge(h_out[a4], o.turn(SLOTS, 1) * 16)
                            dve.wait_ge(scattered[a4], o.turn(SLOTS, 1) * (16 * TOP))
                            dve.wait_ge(h_transposed, o.count(1))
                        dve.tensor_scalar(h_sb[a4][:, 0:D1], resid[a4][:, :], rmv[a2][:, 0:1], rrs[a2][:, 1:2], ALU.subtract,
                                          ALU.mult).then_inc(h_made, 1)
                    if inside(met):
                        s, s4 = met.slot(2), met.slot(SLOTS)
                        dve.wait_ge(ctx_rstd, met.count(1))
                        if met.has(SLOTS):
                            dve.wait_ge(mix_made, met.count(1 - SLOTS))
                        for t in range(3):
                            ins = dve.tensor_scalar(z[s4][:, t, 0:D2], c_sb[s4][:, t, :], mv[s][:, t, 0:1],
                                                    rs[s][:, 1, t:t + 1], ALU.subtract, ALU.mult)
                        ins.then_inc(ctx_norm, 1)
                    if inside(routed):
                        dve.wait_ge(top_vals, routed.count(1))
                        alone(dve)
                        dve.max_index(idx8[r2][:, :], rec[r2][:, NE:NE + 8], rec[r2][:, 0:NE]).then_inc(top_idx, 1)
                    if inside(met):
                        s, s4 = met.slot(2), met.slot(SLOTS)
                        if met.has(2):
                            dve.wait_ge(x_transposed, met.count(-1))
                        dve.tensor_scalar(z1[s][:, :], x_sb[s4][:, :], mv[s][0:LQ, 3, 0:1], rs[s][0:LQ, 1, 3:4],
                                          ALU.subtract, ALU.mult).then_inc(x_norm, 1)
                    if inside(routed):
                        dve.wait_ge(top_idx, routed.count(1))
                        dve.tensor_copy(chosen, idx8[r2][:, 0:TOP]).then_inc(idx_float, 1)
                    if inside(new):
                        dve.wait_ge(x_in[n4], new.turn(SLOTS, 1) * 16)
                        dve.bn_stats(x6[n2][:, :], x_sb[n4][:, :]).then_inc(x_stat6, 1)
                    if inside(routed):
                        dve.wait_ge(idx_float, routed.count(1))
                        dve.tensor_tensor(picks[r2][:, :, :], iota_e[:, :].unsqueeze(1).to_broadcast([LQ, TOP, NE]),
                                          chosen.unsqueeze(2).to_broadcast([LQ, TOP, NE]),
                                          ALU.is_equal).then_inc(picks_made, 1)
                    if inside(new):
                        dve.wait_ge(ctx_stat6, new.count(1))
                        dve.wait_ge(x_stat6, new.count(1))
                        alone(dve)
                        for t in range(3):
                            dve.bn_aggr(mv[n2][:, t, :], c6[n2][:, t, :])
                        dve.bn_aggr(mv[n2][0:LQ, 3, :], x6[n2][:, :]).then_inc(ctx_stats, 1)
                    if inside(routed):
                        dve.wait_ge(picks_made, routed.count(1))
                        with nc.allow_low_precision(reason="zeros and ones"):
                            dve.tensor_reduce(mask[r2][:, :], picks[r2][:, :, :].rearrange("p k e -> p e k"), AX.X,
                                              ALU.add).then_inc(mask_made, 1)
                    if inside(rated):
                        s = rated.slot(2)
                        dve.wait_ge(scores_made, rated.count(1))
                        dve.tensor_reduce(negmax[s][:, :], bank[s][0:LQ, 0:LK], AX.X, ALU.max, negate=True)\
                           .then_inc(rowmax_made, 1)
                    if inside(mixed):
                        dve.wait_ge(probs_made, mixed.count(1))
                        dve.reciprocal(rinv[m2][:, :], rowsum[m2][:, :]).then_inc(rinv_made, 1)
                    if inside(mixed):
                        dve.wait_ge(rinv_made, mixed.count(1))
                        dve.wait_ge(attn_made, mixed.count(1))
                        dve.wait_ge(xr_in[m4], mixed.turn(SLOTS, 1) * 16)
                        if mixed.has(SLOTS):
                            dve.wait_ge(base_out[m4], mixed.turn(SLOTS) * 16)
                        dve.scalar_tensor_tensor(resid[m4][:, :], attn_ps, rinv[m2][:, 0:1], xr_sb[m4][:, :], ALU.mult,
                                                 ALU.add).then_inc(resid_made, 1)
                    if inside(routed):
                        dve.wait_ge(rank_made, routed.count(1))
                        dve.tensor_tensor(slotf[r2][:, :], rank_ps, iota_slot[0:LQ, :], ALU.add).then_inc(slot_sum, 1)
                    if inside(mixed):
                        dve.wait_ge(resid_made, mixed.count(1))
                        dve.bn_stats(r6[m2][:, :], resid[m4][:, :]).then_inc(resid_stat6, 1)
                    if inside(routed):
                        dve.wait_ge(slot_sum, routed.count(1))
                        dve.tensor_tensor(slotp[r2][:, :, :], picks[r2][:, :, :],
                                          slotf[r2][:, :].unsqueeze(1).to_broadcast([LQ, TOP, NE]),
                                          ALU.mult).then_inc(slot_picks, 1)
                    if inside(mixed):
                        dve.wait_ge(resid_stat6, mixed.count(1))
                        alone(dve)
                        dve.bn_aggr(rmv[m2][:, :], r6[m2][:, :]).then_inc(resid_stats, 1)
                    if inside(routed):
                        dve.wait_ge(slot_picks, routed.count(1))
                        if routed.has(2):
                            o = routed.back(2)
                            dve.wait_ge(scattered[o.slot(SLOTS)], o.turn(SLOTS, 1) * (16 * TOP))
                        with nc.allow_low_precision(reason="row numbers, exact in float32"):
                            dve.tensor_reduce(slot[r2][:, :], slotp[r2][:, :, :], AX.X, ALU.add).then_inc(slots_made, 1)

                dve.wait_ge(made, MADE)
                for i in (-2, -1):
                    step(At(0, i, UN))
                dve.memset(g2_1[D2B:D2C, :], 1.0).then_inc(dve_chain, 1)
                dve.memset(gates_all[:, :, NE:NE + 1], 1.0).then_inc(dve_chain, 1)
                dve.wait_ge(weights_in, 16 * 19)
                dve.wait_ge(cols_ready, 1)
                dve.tensor_tensor(wk_aug[:, :, D2], bank[0][:, 0:2], bk_s[:, :], ALU.add)
                dve.tensor_tensor(wv_aug[:, :, D2], bank[0][:, 2:4], bv_s[:, :], ALU.add)
                dve.tensor_tensor(uq[:, :], bank[0][:, 4:6], bq_s[:, :], ALU.add).then_inc(aug_ready, 1)
                dve.wait_ge(folds_made, 1)
                dve.wait_ge(dve_chain, 2)
                for a in range(2):
                    dve.tensor_scalar(fold_q[:, a, :], bank[1][:, a * 256:a * 256 + D2 + 1], g1_s[:, a:a + 1],
                                      (1.0 + EPS) ** -0.5, ALU.mult, ALU.mult)
                dve.tensor_scalar(qs0[:, 0:1], g2_0[:, :], SCALE, None, ALU.mult)
                dve.tensor_scalar(qs1[:, 0:1], g2_1[:, :], SCALE, None, ALU.mult)
                dve.tensor_scalar(fold_o0[:, :], bank[2][:, 0:D1], g2_0[:, :], None, ALU.mult)
                dve.tensor_scalar(fold_o1[:, :], bank[2][0:D2C, D1:2 * D1], g2_1[:, :], None, ALU.mult).then_inc(dve_chain, 1)
                dve.wait_ge(dve_chain, 3)
                dve.tensor_tensor(qs0[:, 1:2], bank[3][:, 0:1], qs0[:, 0:1], ALU.mult)
                dve.tensor_tensor(qs1[:, 1:2], bank[3][0:D2C, 1:2], qs1[:, 0:1], ALU.mult)
                dve.tensor_tensor(fold_o1[D2B:D2C, :], fold_o1[D2B:D2C, :], bo_row[D2B:D2C, :], ALU.add).then_inc(folds_ready, 1)
                dve.wait_ge(small_in, 64)

                walk(dve, step, 0, B + 4, UN, head=8, tail=8)

            @block.tensor
            def _(pe):
                pe.wait_ge(weights_in, 16 * 19)
                for m in range(2):
                    cut = slice(m * P, m * P + P)
                    pe.matmul(bank[0][:, m:m + 1], wk0[:, cut], b2_0[:, :], start=True, stop=False)
                    pe.matmul(bank[0][:, m:m + 1], wk1[:, cut], b2_1[:, :], start=False, stop=True)
                    pe.matmul(bank[0][:, 2 + m:3 + m], wv0[:, cut], b2_0[:, :], start=True, stop=False)
                    pe.matmul(bank[0][:, 2 + m:3 + m], wv1[:, cut], b2_1[:, :], start=False, stop=True)
                    pe.matmul(bank[0][:, 4 + m:5 + m], wq_s[:, 0, cut], b1_s[:, 0:1], start=True, stop=False)
                    mm = pe.matmul(bank[0][:, 4 + m:5 + m], wq_s[:, 1, cut], b1_s[:, 1:2], start=False, stop=True)
                mm.then_inc(cols_ready, 1)
                pe.wait_ge(aug_ready, 1)
                for a in range(2):
                    for c in range(2):
                        pe.matmul(bank[1][:, a * 256:a * 256 + D2 + 1], wqt_s[:, c, a * P:a * P + P], wk_aug[:, c, :],
                                  start=(c == 0), stop=(c == 1))
                for c in range(2):
                    pe.matmul(bank[2][:, 0:D1], wv_aug[:, c, 0:P], wo_s[:, c, :], start=(c == 0), stop=(c == 1))
                for c in range(2):
                    pe.matmul(bank[2][0:D2C, D1:2 * D1], wv_aug[:, c, P:D2 + 1], wo_s[:, c, :], start=(c == 0), stop=(c == 1))
                for c in range(2):
                    pe.matmul(bank[3][:, 0:1], wk_aug[:, c, 0:P], uq[:, c:c + 1], start=(c == 0), stop=(c == 1))
                for c in range(2):
                    mm = pe.matmul(bank[3][0:D2C, 1:2], wk_aug[:, c, P:D2 + 1], uq[:, c:c + 1], start=(c == 0), stop=(c == 1))
                mm.then_inc(folds_made, 1)
                pe.wait_ge(folds_ready, 1)
                pe.wait_ge(made, MADE)
                pe.wait_ge(small_in, 64)

                def step(i):
                    b = i.back(2)
                    if inside(b):
                        s = b.slot(2)
                        pe.wait_ge(probs_made, b.count(1))
                        pe.wait_ge(probs_t_copied, b.count(0))
                        if b.has(3):
                            pe.wait_ge(slot_sum, b.count(-2))
                        for t in range(3):
                            k = KT[t]
                            mm = pe.transpose(probs_ps[0:k, t * LQ:(t + 1) * LQ], probs[s][:, t * P:t * P + k], ident[0:LQ, 0:LQ])
                        mm.then_inc(probs_transposed, 1)
                    b = i
                    if inside(b):
                        s = b.slot(2)
                        pe.wait_ge(x_norm, b.count(1))
                        pe.wait_ge(q_copied, b.count(0))
                        for c in range(2):
                            mm = pe.transpose(z1_ps[:, c * LQ:(c + 1) * LQ], z1[s][:, c * P:c * P + P], ident[0:LQ, 0:LQ])
                        mm.then_inc(x_transposed, 1)
                    b = i
                    if inside(b):
                        s4 = b.slot(SLOTS)
                        pe.wait_ge(ctx_norm, b.count(1))
                        pe.wait_ge(ctx_t_copied, b.count(0))
                        for t in range(3):
                            k = KT[t]
                            pe.transpose(zt_ps0[:, t * P:t * P + k], z[s4][0:k, t, 0:P], ident[0:k, 0:k])
                            mm = pe.transpose(zt_ps1[0:D2C, t * P:t * P + k], z[s4][0:k, t, P:D2 + 1], ident[0:k, 0:k])
                        mm.then_inc(ctx_transposed, 1)
                    b = i.back(2)
                    if inside(b):
                        s, s4 = b.slot(2), b.slot(SLOTS)
                        pe.wait_ge(probs_t_copied, b.count(1))
                        pe.wait_ge(resid_made, b.count(0))
                        for t in range(3):
                            pe.matmul(mix_ps[:, 0:LQ], z[s4][0:KT[t], t, 0:P], probs_t[s][0:KT[t], t, :],
                                      start=(t == 0), stop=(t == 2))
                        for t in range(3):
                            mm = pe.matmul(mix_ps[0:D2C, LQ:2 * LQ], z[s4][0:KT[t], t, P:D2 + 1], probs_t[s][0:KT[t], t, :],
                                           start=(t == 0), stop=(t == 2))
                        mm.then_inc(mix_made, 1)
                    b = i.back(1)
                    if inside(b):
                        s = b.slot(2)
                        pe.wait_ge(ctx_t_copied, b.count(1))
                        pe.wait_ge(q_copied, b.count(1))
                        if b.has(2):
                            pe.wait_ge(probs_made, b.count(-1))
                        pe.matmul(bank[s][0:LQ, 0:LK], qt0[s][:, :], zt0[s][:, :], start=True, stop=False)
                        pe.matmul(bank[s][0:LQ, 0:LK], qt1[s][:, :], zt1[s][:, :], start=False, stop=True)\
                          .then_inc(scores_made, 1)
                    b = i.back(2)
                    if inside(b):
                        s = b.slot(2)
                        pe.wait_ge(mix_copied, b.count(1))
                        pe.matmul(attn_ps, mix0[s][:, :], fold_o0[:, :], start=True, stop=False)
                        pe.matmul(attn_ps, mix1[s][:, :], fold_o1[:, :], start=False, stop=True).then_inc(attn_made, 1)
                    b = i.back(3)
                    if inside(b):
                        s4 = b.slot(SLOTS)
                        pe.wait_ge(h_made, b.count(1))
                        pe.wait_ge(logit_sum, b.count(0))
                        for c in range(2):
                            mm = pe.transpose(h_ps[:, c * LQ:(c + 1) * LQ], h_sb[s4][:, c * P:c * P + P], ident[0:LQ, 0:LQ])
                        mm.then_inc(h_transposed, 1)
                    b = i.back(4)
                    if inside(b):
                        s = b.slot(2)
                        pe.wait_ge(mask_made, b.count(1))
                        pe.wait_ge(msum_made, b.count(0))
                        pe.matmul(rank_ps, tri[:, :], mask[s][:, :], start=True, stop=False)
                        pe.matmul(rank_ps, ones[:, 0:LQ], msum[s][:, :], start=False, stop=True).then_inc(rank_made, 1)
                    b = i
                    if inside(b):
                        s = b.slot(2)
                        pe.wait_ge(x_t_copied, b.count(1))
                        for c in range(2):
                            pe.matmul(q_ps[:, 0:LQ], fold_q[:, c, 0:P], z1t[s][:, c * LQ:(c + 1) * LQ],
                                      start=(c == 0), stop=(c == 1))
                        for c in range(2):
                            mm = pe.matmul(q_ps[0:D2C, LQ:2 * LQ], fold_q[:, c, P:D2 + 1], z1t[s][:, c * LQ:(c + 1) * LQ],
                                           start=(c == 0), stop=(c == 1))
                        mm.then_inc(q_made, 1)
                    b = i.back(3)
                    if inside(b):
                        s = b.slot(2)
                        pe.wait_ge(h_t_copied, b.count(1))
                        for c in range(2):
                            mm = pe.matmul(logit_ps, h_t[s][:, c * LQ:(c + 1) * LQ], wr_s[:, c, :], start=(c == 0), stop=(c == 1))
                        mm.then_inc(logits_made, 1)

                walk(pe, step, 0, B + 4, UN, head=8, tail=4)

        XS = 8
        tile_in = sems(*[f"tile_in{s}" for s in range(XS)])
        y_out = sems(*[f"y_out{s}" for s in range(XS)])
        (tile_transposed, tile_t_copied, w1_ready, up_made, act_made, down_made, y_made) = sems(
            "tile_transposed", "tile_t_copied", "w1_ready", "up_made", "act_made", "down_made", "y_made")
        added = sems("added0", "added1")
        rows_in = sems(*[f"rows_in{s}" for s in range(SLOTS)])
        final_out = sems("final_out0", "final_out1")
        (spare_ready, token_ready, picked, inverse_made, gate_made, gates_copied, gates_transposed, gates_t_copied,
         bias_made, sum_made, final_made) = sems(
            "spare_ready", "token_ready", "picked", "inverse_made", "gate_made", "gates_copied", "gates_transposed",
            "gates_t_copied", "bias_made", "sum_made", "final_made")

        with ExitStack() as st2:
            def s2(name, shape, dt=F32):
                return sb(name, shape, dt, st2)

            NT = SHARED_TILES + ROUTED_TILES
            W = XS
            TABLE_AT = 6
            LEAD = 6
            xt = [s2(f"xt{i}", [P, ROW]) for i in range(XS)]
            y_sb = [s2(f"y_sb{i}", [P, D1]) for i in range(XS)]
            xtt = [s2(f"xtt{i}", [P, 2 * P]) for i in range(2)]
            up = [s2(f"up{i}", [P, 2 * P]) for i in range(2)]
            w1b = [s2(f"w1b{i}", [P, 2 * INTER]) for i in range(2)]
            pick_w, mask_w = s2("pick_w", [LQ, B * TOP, NE]), s2("mask_w", [LQ, B, NE])
            LATE = 22
            gsum = s2("gsum", [LQ, B])
            cnt_i, cnt_s = s2("cnt_i", [P, NE], I32), s2("cnt_s", [P, NE], I32)
            ntile, cum, below, unit = (s2(n, [P, NE]) for n in ("ntile", "cum", "below", "unit"))
            tcol, tab_s = s2("tcol", [P, 8]), s2("tab_s", [P, 2], I32)
            tile_i, tile_e = s2("tile_i", [P, ROUTED_TILES], I32), s2("tile_e", [P, ROUTED_TILES])
            token = [s2(f"token{i}", [P, 1], I32) for i in range(2)]
            own_exp = [s2(f"own_exp{i}", [P, TOP]) for i in range(2)]
            gate, inverse = ([s2(f"{n}{i}", [P, 1]) for i in range(2)] for n in ("gate", "inverse"))
            gb = [s2(f"gb{i}", [LQ, 2 * (NE + 1)]) for i in range(2)]
            gt = [s2(f"gt{i}", [NE + 1, 2 * LQ]) for i in range(2)]
            part0, part1 = ([s2(f"{n}_{i}", [LQ, 2, D1]) for i in range(SLOTS)] for n in ("part0", "part1"))
            final = [s2(f"final{i}", [LQ, 2, D1]) for i in range(2)]

            tile_ps = [bank[0][:, 0:2 * P], bank[1][:, 0:2 * P]]
            up_ps = [bank[2][:, 0:2 * P], bank[3][:, 0:2 * P]]
            down_ps = [bank[4][:, 0:D1], bank[5][:, 0:D1]]
            gt_ps = [bank[0][0:NE + 1, 0:2 * LQ], bank[1][0:NE + 1, 0:2 * LQ]]
            bias_ps = [bank[2][0:LQ, 0:2 * D1], bank[3][0:LQ, 0:2 * D1]]

            def table_entry(eng, t, col, top):
                return eng.value_load(table[0:1, col:col + 1, bass.ds(t.count(-SHARED_TILES), 1)].rearrange("a b c -> a (b c)"),
                                      min_val=0 if col == 0 else TOKENS, max_val=top)

            def adds(t, back=0):
                s = t.slot(2)
                return t.turn(2, 1 - len(range(s, SHARED_TILES, 2)) - back // 2) * 16

            block = st2.enter_context(nc.Block())

            @block.sync
            def _(sp):
                def load(t, routed):
                    s = t.slot(XS)
                    if t.has(XS):
                        sp.wait_ge(y_made, t.count(1 - XS))
                    if t.has(XS + SHARED_TILES):
                        alone(sp)
                        sp.wait_ge(token_ready, t.count(1 - XS - SHARED_TILES))
                    alone(sp)
                    if routed:
                        first = table_entry(sp, t, 1, LIST_END)
                        sp.dma_start(xt[s][:, :], xs[bass.ds(first, P), :]).then_inc(tile_in[s], 16)
                    else:
                        sp.dma_start(xt[s][:, 0:D1], xs[bass.ds(t.count() * P, P), 0:D1]).then_inc(tile_in[s], 16)

                def store(t):
                    s = t.slot(XS)
                    sp.wait_ge(y_made, t.count(1))
                    alone(sp)
                    sp.dma_start(sums[1][bass.ds(t.count() * P, P), :], y_sb[s][:, :]).then_inc(y_out[s], 16)

                def both(t):
                    load(t.back(-LEAD), False)
                    store(t)

                for s in range(SLOTS):
                    sp.wait_ge(h_out[s], B // SLOTS * 16)
                for t in range(LEAD):
                    load(At(0, t, W), False)
                for k in range(2):
                    sp.dma_start(sums[k][TOKENS:TOKENS + P, :], pad_rows[:, 0:D1]).then_inc(spare_ready, 16)
                for t in range(TABLE_AT):
                    both(At(0, t, W))
                sp.wait_ge(table_made, 1)
                with nc.allow_non_contiguous_dma(reason="a small table turned on its side"):
                    sp.dma_start(tab_d.rearrange("n t -> t n"), tab_s[0:ROUTED_TILES, :]).then_inc(table_out, 16)
                for t in range(TABLE_AT, TABLE_AT + 2):
                    both(At(0, t, W))
                sp.wait_ge(table_out, 16)
                sp.dma_start(table[0:1, :, :], tab_d.rearrange("(o n) t -> o n t", o=1)).then_inc(table_in, 16)
                sp.dma_start(tile_i[:, :], tab_d[0, :].partition_broadcast(P)).then_inc(table_in, 16)
                walk(sp, both, TABLE_AT + 2, SHARED_TILES - LEAD, W)
                for s in range(SLOTS):
                    sp.wait_ge(scattered[s], B // SLOTS * TOP * 16)
                sp.wait_ge(pads_out, (NE + 1) * 16)
                sp.wait_ge(table_in, 32)
                for t in range(SHARED_TILES - LEAD, SHARED_TILES):
                    load(At(0, t + LEAD, W), True)
                    store(At(0, t, W))
                walk(sp, lambda t: load(t, True), SHARED_TILES + LEAD, NT, W, head=2)

                for s in range(2):
                    sp.wait_ge(added[s], adds(At(0, NT - 1 - (NT - 1 - s) % 2, W)))

                def pair(dram, b):
                    return dram[0:TOKENS, :].rearrange("(q k p) n -> q p k n", k=2, p=LQ)[bass.ds(b.count(), 1)]\
                        .rearrange("o p k n -> (o p) k n")

                def put(b):
                    s = b.slot(2)
                    sp.wait_ge(final_made, b.count(1))
                    alone(sp)
                    sp.dma_start(pair(out.rearrange("b t d -> (b t) d"), b), final[s][:, :, :]).then_inc(final_out[s], 16)

                def fetch(b):
                    s = b.slot(SLOTS)
                    if b.has(SLOTS):
                        sp.wait_ge(final_made, b.count(1 - SLOTS))
                        alone(sp)
                    sp.dma_start(part0[s][:, :, :], pair(sums[0], b)).then_inc(rows_in[s], 16)
                    sp.dma_start(part1[s][:, :, :], pair(sums[1], b)).then_inc(rows_in[s], 16)

                def both_ways(b):
                    fetch(b)
                    put(b.back(3))

                for b in range(3):
                    fetch(At(0, b, SLOTS))
                walk(sp, both_ways, 3, B // 2, SLOTS, head=1)
                for b in range(B // 2 - 3, B // 2):
                    put(At(0, b, SLOTS))
                for s in range(2):
                    sp.wait_ge(final_out[s], B // 4 * 16)

            @block.gpsimd
            def _(pool):
                pool.dma_start(xs[LIST_END:LIST_END + P, :], pad_rows[:, :]).then_inc(pads_out, 16)
                pool.wait_ge(pads_ready, 1)
                with pool.Fori(0, NE) as e:
                    row = pool.value_load(pad_row[0:1, bass.ds(e, 1)], min_val=TOKENS, max_val=LIST_END - P)
                    pool.dma_start(xs[bass.ds(row, P), :], pad_rows[:, :]).then_inc(pads_out, 16)

                for s in range(SLOTS):
                    pool.wait_ge(base_out[s], B // SLOTS * 16)
                for s in range(XS):
                    pool.wait_ge(y_out[s], len(range(s, SHARED_TILES, XS)) * 16)
                pool.wait_ge(spare_ready, 32)

                def add(t):
                    s, sx = t.slot(2), t.slot(XS)
                    pool.wait_ge(tile_in[sx], t.turn(XS, 1) * 16)
                    if t.has(SHARED_TILES + 2):
                        pool.wait_ge(added[s], adds(t, 2))
                    alone(pool)
                    pool.tensor_copy(token[s][:, :], xt[sx][:, TOKEN:TOKEN + 1]).then_inc(token_ready, 1)
                    pool.wait_ge(token_ready, t.count(1 - SHARED_TILES))
                    pool.wait_ge(y_made, t.count(1))
                    alone(pool)
                    pool.indirect_dma_start(sums[s], bass.IndirectOffsetOnAxis(ap=token[s][:, 0:1], axis=0),
                                            y_sb[sx][:, :], None, compute_op=ALU.add).then_inc(added[s], 16)

                walk(pool, add, SHARED_TILES, NT, W, head=2)

            @block.scalar
            def _(act):
                act.wait_ge(small_in, 64)

                def copy_t(t):
                    s = t.slot(2)
                    act.wait_ge(tile_transposed, t.count(1))
                    if t.has(2):
                        act.wait_ge(up_made, t.count(-1))
                    act.activation(xtt[s][:, :], tile_ps[s], ACT.Copy).then_inc(tile_t_copied, 1)

                def gelu(t, routed):
                    s = t.slot(2)
                    e = bass.ds(table_entry(act, t, 0, NE - 1) if routed else NE, 1)
                    act.wait_ge(up_made, t.count(1))
                    if t.has(2):
                        act.wait_ge(down_made, t.count(-1))
                    for m in range(2):
                        ins = act.activation(up[s][:, m * P:m * P + P], up_ps[s][:, m * P:m * P + P], ACT.Gelu,
                                             bias=b1_all[:, e, m:m + 1].rearrange("p o n -> p (o n)"))
                    ins.then_inc(act_made, 1)

                def both(routed):
                    def step(t):
                        copy_t(t.back(-1))
                        gelu(t, routed)
                    return step

                copy_t(At(0, 0, W))
                walk(act, both(False), 0, SHARED_TILES, W, head=2)
                act.wait_ge(table_in, 32)
                walk(act, both(True), SHARED_TILES, NT - 1, W)
                gelu(At(0, NT - 1, W), True)

                def gates(b):
                    s = b.slot(2)
                    act.wait_ge(gates_transposed, b.count(1))
                    if b.has(2):
                        act.wait_ge(bias_made, b.count(-1))
                    act.activation(gt[s][:, :], gt_ps[s], ACT.Copy).then_inc(gates_t_copied, 1)

                walk(act, gates, 0, B // 2, 2, head=2)

            @block.vector
            def _(dve):
                def evac(t):
                    s, sx = t.slot(2), t.slot(XS)
                    dve.wait_ge(down_made, t.count(1))
                    if t.has(SHARED_TILES + XS):
                        dve.wait_ge(added[s], adds(t, XS))
                    else:
                        dve.wait_ge(y_out[sx], t.turn(XS) * 16)
                    dve.wait_ge(inverse_made, t.count(1 - SHARED_TILES))
                    dve.wait_ge(gate_made, t.count(1 - SHARED_TILES))
                    dve.tensor_scalar(y_sb[sx][:, :], down_ps[s], gate[s][:, 0:1], inverse[s][:, 0:1], ALU.mult,
                                      ALU.mult).then_inc(y_made, 1)

                def evac_shared(t):
                    s, sx = t.slot(2), t.slot(XS)
                    dve.wait_ge(down_made, t.count(1))
                    dve.wait_ge(tile_in[sx], t.turn(XS, 1) * 16)
                    if t.has(XS):
                        dve.wait_ge(y_out[sx], t.turn(XS) * 16)
                    dve.tensor_tensor(y_sb[sx][:, :], down_ps[s], xt[sx][:, 0:D1], ALU.add).then_inc(y_made, 1)

                def fetch_w1(n):
                    e = table_entry(dve, n, 0, NE - 1)
                    if n.has(SHARED_TILES + 2):
                        dve.wait_ge(up_made, n.count(-1))
                    dve.tensor_copy(w1b[n.slot(2)][:, :], w1_all[:, bass.ds(e, 1), :].rearrange("p o n -> p (o n)"))\
                       .then_inc(w1_ready, 1)

                def step(t, more=True):
                    s, sx = t.slot(2), t.slot(XS)
                    r = t.count(1 - SHARED_TILES)
                    dve.wait_ge(tile_in[sx], t.turn(XS, 1) * 16)
                    dve.scalar_tensor_tensor(own_exp[s][:, :], xt[sx][:, WHO:WHO + TOP],
                                             tile_e[:, bass.ds(t.count(-SHARED_TILES), 1)], xt[sx][:, EXPS:EXPS + TOP],
                                             ALU.is_equal, ALU.mult).then_inc(picked, 1)
                    dve.reciprocal(inverse[s][:, :], xt[sx][:, SUM:SUM + 1]).then_inc(inverse_made, 1)
                    if more:
                        fetch_w1(t.back(-2))
                    dve.wait_ge(picked, r)
                    dve.tensor_reduce(gate[s][:, :], own_exp[s][:, :], AX.X, ALU.add).then_inc(gate_made, 1)
                    evac(t)

                steps = [0]

                def late(ins, wait=True):
                    steps[0] += 1
                    ins.then_inc(late_steps, 1)
                    if wait:
                        dve.wait_ge(late_steps, steps[0])

                late(dve.memset(unit[:, :], 1.0))
                dve.wait_ge(counts_made, 1)
                counts = bank[6][:, 0:NE]
                late(dve.tensor_scalar(cnt_i[:, :], counts, float(P - 1), None, ALU.add))
                dve.tensor_tensor(pad_row[0:1, :], counts[0:1, :], iota_slot[0:1, :], ALU.add).then_inc(pads_ready, 1)
                late(dve.tensor_scalar(cnt_s[:, :], cnt_i[:, :], P.bit_length() - 1, None, ALU.arith_shift_right))
                late(dve.tensor_copy(ntile[:, :], cnt_s[:, :]))
                late(dve.tensor_tensor_scan(cum[:, :], unit[:, :], ntile[:, :], 0.0, ALU.mult, ALU.add))
                evac_shared(At(0, 0, W))
                late(dve.tensor_scalar(below[:, :], cum[:, :], tile_no[:, :], None, ALU.is_le))
                expert, before, real, own, e2, r0, r1 = (tcol[:, k:k + 1] for k in range(7))
                late(dve.tensor_reduce(expert, below[:, :], AX.X, ALU.add))
                late(dve.tensor_tensor(below[:, :], below[:, :], ntile[:, :], ALU.mult))
                late(dve.tensor_reduce(before, below[:, :], AX.X, ALU.add))
                evac_shared(At(0, 1, W))
                late(dve.tensor_scalar(real, expert, float(NE), None, ALU.is_lt))
                late(dve.tensor_tensor(own, tile_no[:, :], before, ALU.subtract))
                late(dve.tensor_tensor(e2, expert, real, ALU.mult))
                late(dve.tensor_tensor(own, own, real, ALU.mult))
                evac_shared(At(0, 2, W))
                late(dve.tensor_scalar(r0, expert, float(CAP), float(TOKENS), ALU.mult, ALU.add))
                late(dve.tensor_scalar(r1, own, float(P), None, ALU.mult))
                dve.tensor_copy(tab_s[:, 0:1], e2)
                dve.tensor_tensor(tab_s[:, 1:2], r0, r1, ALU.add).then_inc(table_made, 1)
                evac_shared(At(0, 3, W))
                four = [LQ, B, TOP, NE]
                picks4 = pick_w[:, :, :].rearrange("p (b k) e -> p b k e", k=TOP)
                late(dve.tensor_tensor(picks4, idx_all[:, :, :].unsqueeze(3).to_broadcast(four),
                                       iota_e[:, :].unsqueeze(1).unsqueeze(1).to_broadcast(four), ALU.is_equal), wait=False)
                for t in range(4, 6):
                    evac_shared(At(0, t, W))
                dve.wait_ge(late_steps, steps[0])
                late(dve.tensor_reduce(mask_w[:, :, :], picks4.rearrange("p b k e -> p b e k"), AX.X, ALU.add), wait=False)
                for t in range(6, 8):
                    evac_shared(At(0, t, W))
                late(dve.tensor_reduce(gsum[:, :], gates_all[:, :, 0:NE], AX.X, ALU.add))
                late(dve.reciprocal(gsum[:, :], gsum[:, :]))
                late(dve.tensor_tensor(gates_all[:, :, 0:NE], gates_all[:, :, 0:NE], mask_w[:, :, :], ALU.mult), wait=False)
                for t in range(8, 10):
                    evac_shared(At(0, t, W))
                dve.wait_ge(late_steps, steps[0])
                late(dve.tensor_tensor(gates_all[:, :, 0:NE], gates_all[:, :, 0:NE],
                                       gsum[:, :].unsqueeze(2).to_broadcast([LQ, B, NE]), ALU.mult), wait=False)
                walk(dve, evac_shared, 10, SHARED_TILES - 2, W)
                dve.wait_ge(expert_in, 16 * 2 * B)
                dve.wait_ge(table_in, 32)
                late(dve.tensor_copy(tile_e[:, :], tile_i[:, :]))
                assert steps[0] == LATE, steps[0]
                for t in range(SHARED_TILES - 2, SHARED_TILES):
                    fetch_w1(At(0, t + 2, W))
                    evac_shared(At(0, t, W))
                walk(dve, step, SHARED_TILES, NT - 2, W, head=XS)
                for t in range(NT - 2, NT):
                    step(At(0, t, W), more=False)

                def copy_gates(b):
                    s = b.slot(2)
                    if b.has(2):
                        dve.wait_ge(gates_transposed, b.count(-1))
                    dve.tensor_copy(gb[s][:, :], gates_all[:, bass.ds(b.count() * 2, 2), :].rearrange("p k n -> p (k n)"))\
                       .then_inc(gates_copied, 1)

                def combine(b):
                    s, s4 = b.slot(2), b.slot(SLOTS)
                    dve.wait_ge(rows_in[s4], b.turn(SLOTS, 1) * 32)
                    dve.tensor_tensor(part0[s4][:, :, :], part0[s4][:, :, :], part1[s4][:, :, :], ALU.add).then_inc(sum_made, 1)
                    if not b.fixed or b.r < B // 2 - 2:
                        copy_gates(b.back(-2))
                    dve.wait_ge(sum_made, b.count(1))
                    dve.wait_ge(bias_made, b.count(1))
                    if b.has(2):
                        dve.wait_ge(final_out[s], b.turn(2) * 16)
                    dve.tensor_tensor(final[s][:, :, :].rearrange("p k n -> p (k n)"), part0[s4][:, :, :].rearrange("p k n -> p (k n)"),
                                      bias_ps[s], ALU.add).then_inc(final_made, 1)

                for b in range(2):
                    copy_gates(At(0, b, SLOTS))
                walk(dve, combine, 0, B // 2, SLOTS, head=2, tail=2)

            @block.tensor
            def _(pe):
                pe.wait_ge(expert_in, 16 * 2 * B)
                pe.matmul(bank[6][:, 0:NE], ones[:, :], msum[B % 2][:, :], start=True, stop=True).then_inc(counts_made, 1)

                def transposes(t):
                    s, sx = t.slot(2), t.slot(XS)
                    pe.wait_ge(tile_in[sx], t.turn(XS, 1) * 16)
                    if t.has(2):
                        pe.wait_ge(tile_t_copied, t.count(-1))
                    for c in range(2):
                        mm = pe.transpose(tile_ps[s][:, c * P:c * P + P], xt[sx][:, c * P:c * P + P], ident[:, :])
                    mm.then_inc(tile_transposed, 1)

                def up_product(t, routed):
                    s = t.slot(2)
                    pe.wait_ge(tile_t_copied, t.count(1))
                    if t.has(2):
                        pe.wait_ge(act_made, t.count(-1))
                    if routed:
                        pe.wait_ge(w1_ready, t.count(1 - SHARED_TILES))
                    w = w1b[s] if routed else w1_all[:, NE, :]
                    for m in range(2):
                        for c in range(2):
                            mm = pe.matmul(up_ps[s][:, m * P:m * P + P], w[:, c * INTER + m * P:c * INTER + m * P + P],
                                           xtt[s][:, c * P:c * P + P], start=(c == 0), stop=(c == 1))
                    mm.then_inc(up_made, 1)

                def down_product(t, routed):
                    s = t.slot(2)
                    e = bass.ds(table_entry(pe, t, 0, NE - 1) if routed else NE, 1)
                    pe.wait_ge(act_made, t.count(1))
                    if t.has(2):
                        pe.wait_ge(y_made, t.count(-1))
                    for m in range(2):
                        w = w2_all[:, e, m * D1:(m + 1) * D1].rearrange("p o n -> p (o n)")
                        mm = pe.matmul(down_ps[s], up[s][:, m * P:m * P + P], w, start=(m == 0), stop=(m == 1))
                    mm.then_inc(down_made, 1)

                def three(up_routed, down_routed):
                    def step(t):
                        transposes(t.back(-2))
                        up_product(t.back(-1), up_routed)
                        down_product(t, down_routed)
                    return step

                transposes(At(0, 0, W))
                transposes(At(0, 1, W))
                up_product(At(0, 0, W), False)
                walk(pe, three(False, False), 0, SHARED_TILES - 1, W, head=2)
                pe.wait_ge(table_in, 32)
                three(True, False)(At(0, SHARED_TILES - 1, W))
                walk(pe, three(True, True), SHARED_TILES, NT - 2, W)
                up_product(At(0, NT - 1, W), True)
                down_product(At(0, NT - 2, W), True)
                down_product(At(0, NT - 1, W), True)

                def turn_gates(b):
                    s = b.slot(2)
                    pe.wait_ge(gates_copied, b.count(1))
                    if b.has(2):
                        pe.wait_ge(gates_t_copied, b.count(-1))
                    for k in range(2):
                        mm = pe.transpose(gt_ps[s][:, k * LQ:(k + 1) * LQ], gb[s][:, k * (NE + 1):(k + 1) * (NE + 1)],
                                          ident[0:LQ, 0:LQ])
                    mm.then_inc(gates_transposed, 1)

                def bias_rows(b):
                    s = b.slot(2)
                    if not b.fixed or b.r < B // 2 - 1:
                        turn_gates(b.back(-1))
                    pe.wait_ge(gates_t_copied, b.count(1))
                    if b.has(2):
                        pe.wait_ge(final_made, b.count(-1))
                    for k in range(2):
                        mm = pe.matmul(bias_ps[s][:, k * D1:(k + 1) * D1], gt[s][:, k * LQ:(k + 1) * LQ], b2_all[:, :],
                                       start=True, stop=True)
                    mm.then_inc(bias_made, 1)

                turn_gates(At(0, 0, 2))
                walk(pe, bias_rows, 0, B // 2, 2, head=2, tail=2)


def kernel(**inputs):
    import numpy as np
    import concourse.bacc as bacc
    from concourse.bass_utils import run_bass_kernel_spmd

    get = {k.replace("L0_xattn_", "").replace("L0_ffn_", "ffn_"): np.asarray(v) for k, v in inputs.items()}

    def column(v, n=2):
        return v.reshape(n, -1).T

    def expert(shared, each):
        w = np.concatenate([each, shared[None]])
        return w.reshape(w.shape[0], 2, P, w.shape[2]).transpose(0, 2, 1, 3).reshape(w.shape[0], P, -1)

    be1 = np.concatenate([get["ffn_Be1"], get["ffn_bs1"][None]])
    arrays = {
        "x": get["x"], "ctx": get["ctx_768"],
        "g1c": column(get["ln1_g"]), "b1c": column(get["ln1_b"]),
        "g2c": get["ln2_g"][:, None], "b2c": get["ln2_b"][:, None],
        "wq": get["Wq"], "wqt": get["Wq"].T, "bqc": column(get["bq"]),
        "wk": get["Wk"], "wkt": get["Wk"].T, "bkc": column(get["bk"]),
        "wv": get["Wv"], "wvt": get["Wv"].T, "bvc": column(get["bv"]),
        "wo": get["Wo"], "bo": get["bo"][None],
        "w1": expert(get["ffn_ws1"], get["ffn_We1"]),
        "be1": be1.reshape(NE + 1, 2, P).transpose(2, 0, 1),
        "w2": expert(get["ffn_ws2"], get["ffn_We2"]),
        "b2": np.concatenate([get["ffn_Be2"], get["ffn_bs2"][None]]),
        "wr": get["ffn_Wr"], "br": get["ffn_br"],
    }
    nc = bacc.Bacc("TRN2", target_bir_lowering=False, num_devices=1)
    args, given = [], {}
    for name, a in arrays.items():
        a = np.ascontiguousarray(a)
        given[f"in_{name}"] = a
        args.append(nc.dram_tensor(f"in_{name}", a.shape, mybir.dt.from_np(a.dtype), kind="ExternalInput").ap())
    args.append(nc.dram_tensor("out_0", (B, LQ, D1), F32, kind="ExternalOutput").ap())
    program(nc, *args)
    r = run_bass_kernel_spmd(nc, [given], core_ids=[0])
    return r.results[0]["out_0"]
```
